# Optimizing a Trainium2 kernel written in Bass

```python
import numpy as np
import jax
import jax.numpy as jnp

def _softmax(x, axis=-1):
    return jax.nn.softmax(x, axis=axis)

def _gelu(x):
    return jax.nn.gelu(x, approximate=True)

def _silu(x):
    return jax.nn.silu(x)

def _sigmoid(x):
    return jax.nn.sigmoid(x)

def _layernorm(x, axis=-1, eps=1e-05):
    m = jnp.mean(x, axis=axis, keepdims=True)
    v = jnp.var(x, axis=axis, keepdims=True)
    return (x - m) / jnp.sqrt(v + eps)

def _scatter_add(tgt, idx, src, axis=0):
    return tgt.at[idx].add(src)

def _segment_sum(src, seg, n):
    return jax.ops.segment_sum(src, seg, n)
kernel_name = 'mk_gnn_resnorm_d1_gnn_r8_71a1ea'

def setup_inputs(seed: int=0):
    np.random.seed(seed)
    _w = jnp.asarray

    def _rec_inputs():
        import jax
        import jax.numpy as jnp
        _gk = jax.random.key(seed)
        x = 0.0001712 + 1 * jax.random.normal(jax.random.fold_in(_gk, 1), (12500, 16), jnp.float32)
        src = jax.random.randint(jax.random.fold_in(_gk, 2), (400000,), 0, 12500, jnp.int32)
        dst = jnp.minimum((12500 * jax.random.uniform(jax.random.fold_in(_gk, 3), (400000,)) ** 2.0).astype(jnp.int32), 99999)
        _o = jnp.argsort(dst, stable=True)
        src = src[_o]
        dst = dst[_o]
        edge_attr_13 = 2.91757e-06 + 0.999892 * jax.random.normal(jax.random.fold_in(_gk, 12), (400000, 13), jnp.float32)
        return (x, src, dst, edge_attr_13)
    x, src, dst, edge_attr_13 = _rec_inputs()

    def _L0_gnn_setup():
        import jax, jax.numpy as jnp
        import numpy as np
        N = 6250
        E = 100000
        NC = 16
        FDIM = 13
        HID = 32
        NREPEATS = 2

        def _gru_cell(x, h, w_ih, w_hh, b_ih, b_hh):
            gi = x @ w_ih.T + b_ih
            gh = h @ w_hh.T + b_hh
            i_r, i_z, i_n = jnp.split(gi, 3, axis=1)
            h_r, h_z, h_n = jnp.split(gh, 3, axis=1)
            r = jax.nn.sigmoid(i_r + h_r)
            z = jax.nn.sigmoid(i_z + h_z)
            n = jnp.tanh(i_n + r * h_n)
            return (1.0 - z) * n + z * h
        key = jax.random.key(seed)
        ks = jax.random.split(key, 10)
        hx = jax.random.normal(ks[0], (N, NC), dtype=jnp.float32)
        edgefeats = jax.random.normal(ks[1], (E, FDIM), dtype=jnp.float32)
        edge_src = jax.random.randint(ks[2], (E,), 0, N, dtype=jnp.int32)
        edge_dst = jax.random.randint(ks[3], (E,), 0, N, dtype=jnp.int32)
        fnet_w1 = jax.random.normal(ks[4], (FDIM, HID), dtype=jnp.float32) * (1.0 / np.sqrt(FDIM))
        fnet_b1 = jnp.zeros((HID,), dtype=jnp.float32)
        fnet_w2 = jax.random.normal(ks[5], (HID, NC * NC), dtype=jnp.float32) * (0.1 / np.sqrt(HID))
        fnet_b2 = jnp.zeros((NC * NC,), dtype=jnp.float32)
        gru_w_ih = jax.random.normal(ks[6], (3 * NC, NC), dtype=jnp.float32) * (1.0 / np.sqrt(NC))
        gru_w_hh = jax.random.normal(ks[7], (3 * NC, NC), dtype=jnp.float32) * (1.0 / np.sqrt(NC))
        gru_b_ih = jnp.zeros((3 * NC,), dtype=jnp.float32)
        gru_b_hh = jnp.zeros((3 * NC,), dtype=jnp.float32)
        return {'hx': hx, 'edgefeats': edgefeats, 'edge_src': edge_src, 'edge_dst': edge_dst, 'fnet_w1': fnet_w1, 'fnet_b1': fnet_b1, 'fnet_w2': fnet_w2, 'fnet_b2': fnet_b2, 'gru_w_ih': gru_w_ih, 'gru_w_hh': gru_w_hh, 'gru_b_ih': gru_b_ih, 'gru_b_hh': gru_b_hh}
    _L0_gnn_all = _L0_gnn_setup()
    _L0_gnn_in = {k: v for k, v in _L0_gnn_all.items() if k in ('fnet_w1', 'fnet_b1', 'fnet_w2', 'fnet_b2', 'gru_w_ih', 'gru_w_hh', 'gru_b_ih', 'gru_b_hh')}
    del _L0_gnn_all
    return {'x': x, 'src': src, 'dst': dst, 'edge_attr_13': edge_attr_13, 'L0_gnn_fnet_w1': _L0_gnn_in['fnet_w1'], 'L0_gnn_fnet_b1': _L0_gnn_in['fnet_b1'], 'L0_gnn_fnet_w2': _L0_gnn_in['fnet_w2'], 'L0_gnn_fnet_b2': _L0_gnn_in['fnet_b2'], 'L0_gnn_gru_w_ih': _L0_gnn_in['gru_w_ih'], 'L0_gnn_gru_w_hh': _L0_gnn_in['gru_w_hh'], 'L0_gnn_gru_b_ih': _L0_gnn_in['gru_b_ih'], 'L0_gnn_gru_b_hh': _L0_gnn_in['gru_b_hh']}

def reference(x, src, dst, edge_attr_13, L0_gnn_fnet_w1, L0_gnn_fnet_b1, L0_gnn_fnet_w2, L0_gnn_fnet_b2, L0_gnn_gru_w_ih, L0_gnn_gru_w_hh, L0_gnn_gru_b_ih, L0_gnn_gru_b_hh):
    import jax
    import jax.numpy as jnp

    def _L0_gnn_ref(hx, edgefeats, edge_src, edge_dst, fnet_w1, fnet_b1, fnet_w2, fnet_b2, gru_w_ih, gru_w_hh, gru_b_ih, gru_b_hh):
        import jax, jax.numpy as jnp
        import numpy as np
        N = 6250
        E = 100000
        NC = 16
        FDIM = 13
        HID = 32
        NREPEATS = 2

        def _gru_cell(x, h, w_ih, w_hh, b_ih, b_hh):
            gi = x @ w_ih.T + b_ih
            gh = h @ w_hh.T + b_hh
            i_r, i_z, i_n = jnp.split(gi, 3, axis=1)
            h_r, h_z, h_n = jnp.split(gh, 3, axis=1)
            r = jax.nn.sigmoid(i_r + h_r)
            z = jax.nn.sigmoid(i_z + h_z)
            n = jnp.tanh(i_n + r * h_n)
            return (1.0 - z) * n + z * h
        n_nodes, nc = hx.shape
        w = jax.nn.relu(edgefeats @ fnet_w1 + fnet_b1) @ fnet_w2 + fnet_b2
        W = w.reshape(-1, nc, nc)
        deg = jax.ops.segment_sum(jnp.ones((edge_dst.shape[0],), hx.dtype), edge_dst, num_segments=n_nodes)
        inv_deg = 1.0 / jnp.maximum(deg, 1.0)
        for _ in range(NREPEATS):
            xj = hx[edge_src]
            m = jnp.einsum('ei,eio->eo', xj, W)
            agg = jax.ops.segment_sum(m, edge_dst, num_segments=n_nodes)
            agg = agg * inv_deg[:, None]
            hx = _gru_cell(agg, hx, gru_w_ih, gru_w_hh, gru_b_ih, gru_b_hh)
        return hx
    x = _layernorm(x + _L0_gnn_ref(x, edge_attr_13, src, dst, L0_gnn_fnet_w1, L0_gnn_fnet_b1, L0_gnn_fnet_w2, L0_gnn_fnet_b2, L0_gnn_gru_w_ih, L0_gnn_gru_w_hh, L0_gnn_gru_b_ih, L0_gnn_gru_b_hh), axis=-1)
    return x

_drawn_inputs = setup_inputs


def setup_inputs(seed=0):
    import zlib

    import numpy as np

    out = dict(_drawn_inputs(seed))
    spreads = {'L0_gnn_fnet_b1': (0.0, 2.0),
     'L0_gnn_fnet_b2': (0.0, 0.1),
     'L0_gnn_gru_b_ih': (0.0, 0.1),
     'L0_gnn_gru_b_hh': (0.0, 0.1)}
    factors = {'edge_attr_13': 3.022, 'L0_gnn_fnet_w1': 3.017}
    for name, (base, spread) in spreads.items():
        noise = np.random.default_rng([zlib.crc32(name.encode()), seed]).standard_normal(out[name].shape)
        drawn = base * np.exp(spread * noise) if base else spread * noise
        out[name] = jnp.asarray(drawn.astype(out[name].dtype))
    for name, factor in factors.items():
        out[name] = (out[name] * factor).astype(out[name].dtype)
    return out
```

```python
from contextlib import ExitStack

import concourse.bass as bass
from concourse import mybir

P = 128
BANK = 512
F32 = mybir.dt.float32
I32 = mybir.dt.int32
U32 = mybir.dt.uint32
ALU = mybir.AluOpType
ACT = mybir.ActivationFunctionType
AX_X = mybir.AxisListType.X

TPG = 5
GPS = 5
WIN = 64
QUADS = 4
QS = 32
CNT = 32
CREDIT = 16
META = 12
LN_EPS = 1e-5


def gnn_program(nc, x, x_t, src_tiles, dst, dst_tiles, ef_t, w1, b1, w2_oi, b2_oi,
                w_ih_t, w_hh_t, b_ih_g, b_hh_g, out):
    N, C = x.shape
    FD, E = ef_t.shape
    HID = w1.shape[1]
    HA = HID + 1
    WC = C * C
    GE = TPG * P
    HE = GE // 2
    SE = GPS * GE
    TPS = TPG * GPS
    NSUB = E // SE
    NG = NSUB * GPS
    PAIRS, TAIL = NSUB // 2, NSUB % 2
    Q = N // QUADS
    RP = 125
    RJ = Q // RP
    ROUNDS = 2
    GW = 500
    STEPS = [(o, min(GW, Q - o)) for o in range(0, Q, GW)]
    assert E % SE == 0 and NSUB <= P and N % QUADS == 0 and Q % RP == 0 and C == 16

    def uses(rnd, par, i):
        per_round = PAIRS + (TAIL if par == 0 else 0)
        return i + (rnd * per_round + 1)

    table2 = nc.dram_tensor("h_rows", [N, C], F32, kind="Internal").ap()
    meta_d = nc.dram_tensor("meta_d", [NSUB, META], I32, kind="Internal").ap()
    base_d = nc.dram_tensor("base_d", [NSUB, GPS], F32, kind="Internal").ap()

    with ExitStack() as ctx:
        def sb(name, shape, dt=F32):
            return ctx.enter_context(nc.sbuf_tensor(name, shape, dt))

        def ps(name, shape):
            return ctx.enter_context(nc.psum_tensor(name, shape, F32))

        def sem(name):
            return ctx.enter_context(nc.semaphore(name))

        w1_sb = sb("w1_sb", [P, P])
        b1_sb = sb("b1_sb", [P, 1])
        w2_sb = sb("w2_sb", [P, WC])
        gate_w = sb("gate_w", [P, 6, P])
        bias_ih = sb("bias_ih", [P, 3])
        bias_hh = sb("bias_hh", [P, 3])
        bias_rz = sb("bias_rz", [P, 2])
        ident = sb("ident", [P, P])
        win_iota = sb("win_iota", [P, WIN])
        eps = sb("eps", [P, 1])
        dst_nat = sb("dst_nat", [NSUB, SE], I32)
        dst_sb = sb("dst_sb", [P, NSUB * TPS], I32)
        base_all = sb("base_all", [P, NG])
        lo_hi = sb("lo_hi", [NSUB, 2, GPS])
        span = sb("span", [NSUB, GPS], I32)
        meta_w = sb("meta_w", [NSUB, META], I32)
        meta = sb("meta", [1, NSUB * META], I32)
        idx = sb("idx", [P, 2, TPS], I32)
        ef = sb("ef", [P, 2, SE])
        h_sb = sb("h_sb", [P, 2, GE])
        xg = sb("xg", [P, 2 * GPS, TPG, C])
        rel = sb("rel", [P, 2, TPS])
        prod = sb("prod", [P, 2, TPG, C, C])
        hot = sb("hot", [P, 2, TPG, WIN])
        msg = sb("msg", [P, 2 * GPS, TPG, CNT + C])
        rel_x = sb("rel_x", [P, TPG])
        hot_x = sb("hot_x", [P, TPG, WIN])
        acc = sb("acc", [CNT + C, N + WIN])
        hq = sb("hq", [P, Q])
        agg_q = sb("agg_q", [P, 2, GW])
        cnt_q = sb("cnt_q", [P, 2, GW])
        r_q = sb("r_q", [P, GW])
        z_q = sb("z_q", [P, GW])
        t_q = sb("t_q", [P, GW])
        n_q = sb("n_q", [P, GW])
        rows = sb("rows", [RP, QUADS, RJ, C])
        xrows = sb("xrows", [RP, QUADS, RJ, C])
        cent = sb("cent", [RP, QUADS * RJ, C])
        stat = sb("stat", [RP, 4, QUADS * RJ])

        ps_w = ps("ps_w", [P, 6 * BANK])
        ps_h = ps("ps_h", [P, BANK])
        ps_a = ps("ps_a", [P, BANK])
        win_sum = ps_a[0:CNT + C, 0:WIN]
        R_BANK, Z_BANK, IN_BANK, HN_BANK, TR_BANK0 = (BANK * b for b in range(5))

        def w_slot(s):
            return ps_w[:, s * 3 * BANK:s * 3 * BANK + TPG * WC]

        s_const = sem("s_const")
        s_dst = sem("s_dst")
        s_hq = sem("s_hq")
        s_fill = sem("s_fill")
        s_meta_w = sem("s_meta_w")
        s_meta = sem("s_meta")
        s_pro = sem("s_pro")
        s_ef = [sem(f"s_ef{p}") for p in range(2)]
        s_idx = [sem(f"s_idx{p}") for p in range(2)]
        s_xg = [sem(f"s_xg{k}") for k in range(2 * GPS)]
        s_h = sem("s_h")
        s_relu = sem("s_relu")
        s_w = sem("s_w")
        s_rel = sem("s_rel")
        s_prod = sem("s_prod")
        s_hot = sem("s_hot")
        s_msg = sem("s_msg")
        s_agg = sem("s_agg")
        s_acc = sem("s_acc")
        s_hot_x = sem("s_hot_x")
        s_agg_x = sem("s_agg_x")
        s_pack = sem("s_pack")
        s_norm = sem("s_norm")
        s_gate = sem("s_gate")
        s_rz = sem("s_rz")
        s_pre = sem("s_pre")
        s_n = sem("s_n")
        s_new = sem("s_new")
        s_link = sem("s_link")
        s_tr = sem("s_tr")
        s_rows = sem("s_rows")
        s_table = sem("s_table")
        s_zero = sem("s_zero")
        s_ln = sem("s_ln")
        s_sd = sem("s_sd")
        s_y = sem("s_y")
        s_out = sem("s_out")

        N_CONST = 5 + 6 * QUADS + 2 * QUADS
        HQ_LOADS = QUADS + 1
        TR_BANK = BANK // P
        BANKS = -(-RJ // TR_BANK)
        by_row = "(q p j) c -> p q (j c)"

        block = ctx.enter_context(nc.Block())

        def for_subs(eng, emit):
            if PAIRS:
                with eng.Fori(0, PAIRS) as i:
                    emit(i, 0, False)
                    emit(i, 1, TAIL == 0)
            if TAIL:
                emit(PAIRS, 0, True)

        @block.sync
        def _(sp):
            sp.dma_start(dst_nat[:], dst.rearrange("(s e) -> s e", s=NSUB)).then_inc(s_dst, 16)
            sp.dma_start(dst_sb[:], dst_tiles).then_inc(s_dst, 16)
            sp.wait_ge(s_fill, 1)
            sp.dma_start(w1_sb[0:FD, 0:HID], w1).then_inc(s_const, 16)
            sp.dma_start(b1_sb[0:HID, :], b1).then_inc(s_const, 16)
            sp.dma_start(w2_sb[0:HID, :], w2_oi).then_inc(s_const, 16)
            sp.dma_start(w2_sb[HID:HA, :], b2_oi).then_inc(s_const, 16)
            sp.dma_start(xrows[:], x.rearrange(by_row, q=QUADS, p=RP)).then_inc(s_const, 16)
            for q in range(QUADS):
                lo = QS * q
                for side, w in ((0, w_ih_t), (1, w_hh_t)):
                    for g in range(3):
                        sp.dma_start(gate_w[lo:lo + C, 3 * side + g, lo:lo + C],
                                     w[:, g * C:(g + 1) * C]).then_inc(s_const, 16)
                sp.dma_start(bias_ih[lo:lo + C, :], b_ih_g).then_inc(s_const, 16)
                sp.dma_start(bias_hh[lo:lo + C, :], b_hh_g).then_inc(s_const, 16)
                sp.dma_start(hq[lo:lo + C, :], x_t[:, q * Q:(q + 1) * Q]).then_inc(s_hq, 16)
            sp.wait_ge(s_pro, 7)
            sp.dma_start(meta_d, meta_w[:]).then_inc(s_meta_w, 16)
            sp.dma_start(base_d, lo_hi[:, 0, :]).then_inc(s_meta_w, 16)
            sp.wait_ge(s_meta_w, 32)
            sp.dma_start(meta[:], meta_d.rearrange("s m -> (s m)").unsqueeze(0)).then_inc(s_meta, 16)
            sp.dma_start(base_all[:], base_d.rearrange("s g -> (s g)").unsqueeze(0)
                         .to_broadcast([P, NG])).then_inc(s_meta, 16)

            for rnd in range(ROUNDS):
                def emit(i, par, last, rnd=rnd):
                    sub = 2 * i + par
                    done = rnd * NG + (sub - 1) * GPS
                    sp.wait_ge(s_prod, done + CREDIT)
                    sp.dma_start(idx[:, par, :], src_tiles[bass.ds(sub * P, P), :]).then_inc(s_idx[par], 16)
                    sp.wait_ge(s_h, done * 2 + CREDIT)
                    sp.dma_start(ef[0:FD, par, :], ef_t[:, bass.ds(sub * SE, SE)]).then_inc(s_ef[par], 16)

                for_subs(sp, emit)
                if rnd < ROUNDS - 1:
                    sp.wait_ge(s_rows, BANKS * (rnd + 1))
                    sp.dma_start(table2.rearrange(by_row, q=QUADS, p=RP), rows[:]).then_inc(s_table, 16)
            sp.wait_ge(s_y, 1)
            sp.dma_start(out.rearrange(by_row, q=QUADS, p=RP), rows[:]).then_inc(s_out, 16)
            sp.wait_ge(s_out, 16)
            sp.wait_ge(s_table, 16 * (ROUNDS - 1))

        @block.gpsimd
        def _(pool):
            for t, v in ((w1_sb, 0.0), (w2_sb, 0.0), (b1_sb, 0.0), (ef, 0.0), (gate_w, 0.0), (bias_ih, 0.0), (bias_hh, 0.0),
                         (hq, 0.0), (ident, 0.0)):
                pool.memset(t[:], v)
            pool.drain()
            pool.memset(b1_sb[HID:HA, :], 1.0)
            pool.drain().then_inc(s_fill, 1)
            pool.wait_ge(s_fill, 1)
            pool.affine_select(out=ident[:], in_=ident[:], compare_op=ALU.not_equal, fill=1.0, base=0,
                               pattern=[[-1, P]], channel_multiplier=1)
            pool.iota(win_iota[:], [[1, WIN]], base=0, channel_multiplier=0,
                      allow_small_or_imprecise_dtypes=True)
            for t, v in ((eps, LN_EPS), (acc, 0.0), (msg, 1.0), (agg_q, 0.0), (cnt_q, 1.0)):
                pool.memset(t[:], v)
            pool.drain().then_inc(s_fill, 1)

            for rnd in range(ROUNDS):
                table = x if rnd == 0 else table2
                if rnd > 0:
                    pool.wait_ge(s_table, 16 * rnd)

                def emit(i, par, last, rnd=rnd, table=table):
                    pool.wait_ge(s_idx[par], 16 * uses(rnd, par, i))
                    for k in range(GPS):
                        g = (2 * i + par) * GPS + k
                        pool.wait_ge(s_prod, rnd * NG + g - 2 * GPS + 1 + CREDIT)
                        pool.nop(nofuse=True)
                        for t in range(TPG):
                            pool.indirect_dma_start(
                                out=xg[:, par * GPS + k, t, :], out_offset=None, in_=table,
                                in_offset=bass.IndirectOffsetOnAxis(
                                    ap=idx[:, par, k * TPG + t:k * TPG + t + 1].bitcast(U32), axis=0),
                            ).then_inc(s_xg[par * GPS + k], 16)

                for_subs(pool, emit)
                if rnd < ROUNDS - 1:
                    pool.wait_ge(s_pack, len(STEPS) * (rnd + 1))
                    pool.memset(acc[:], 0.0).then_inc(s_zero, 1)

        @block.scalar
        def _(act):
            act.sem_inc(s_relu, CREDIT)
            act.wait_ge(s_const, 16 * N_CONST)
            act.wait_ge(s_fill, 2)

            def pack(rnd, c):
                off, w = STEPS[c]
                k = rnd * len(STEPS) + c
                if c >= 2:
                    act.wait_ge(s_gate, k - 1)
                for q in range(QUADS):
                    cols = slice(q * Q + off, q * Q + off + w)
                    act.copy(agg_q[QS * q:QS * q + C, c % 2, 0:w], acc[0:C, cols])
                    last = act.copy(cnt_q[QS * q:QS * q + C, c % 2, 0:w], acc[CNT:CNT + C, cols])
                last.then_inc(s_pack, 1)

            for rnd in range(ROUNDS):
                def emit(i, par, last, rnd=rnd):
                    for k in range(GPS):
                        g = (2 * i + par) * GPS + k
                        act.wait_ge(s_w, rnd * NG + g - 1 + CREDIT)
                        for half in range(2):
                            act.wait_ge(s_h, (rnd * NG + g) * 2 + half + 1 + CREDIT)
                            act.activation(h_sb[:, (par * GPS + k) % 2, half * HE:(half + 1) * HE],
                                           ps_h[:, 0:HE], ACT.Relu,
                                           bias=b1_sb[:, 0:1]).then_inc(s_relu, 1)

                for_subs(act, emit)
                act.wait_ge(s_acc, NG * (rnd + 1) + CREDIT + rnd + 1)
                pack(rnd, 0)
                for c, (off, w) in enumerate(STEPS):
                    if c + 1 < len(STEPS):
                        pack(rnd, c + 1)
                    k = rnd * len(STEPS) + c
                    act.wait_ge(s_gate, k + 1)
                    act.wait_ge(s_new, k)
                    act.activation(r_q[:, 0:w], ps_w[:, 0:w], ACT.Sigmoid, bias=bias_rz[:, 0:1])
                    act.activation(z_q[:, 0:w], ps_w[:, Z_BANK:Z_BANK + w], ACT.Sigmoid,
                                   bias=bias_rz[:, 1:2]).then_inc(s_rz, 1)
                    act.wait_ge(s_pre, k + 1)
                    act.activation(n_q[:, 0:w], t_q[:, 0:w], ACT.Tanh, bias=bias_ih[:, 2:3]).then_inc(s_n, 1)
            act.wait_ge(s_ln, 1)
            act.activation(stat[:, 2, :], stat[:, 1, :], ACT.Sqrt, bias=eps[0:RP, :],
                           scale=1.0 / C).then_inc(s_sd, 1)

        @block.tensor
        def _(pe):
            pe.sem_inc(s_h, CREDIT)
            pe.sem_inc(s_w, CREDIT)
            pe.sem_inc(s_agg, CREDIT)
            pe.wait_ge(s_const, 16 * N_CONST)
            pe.wait_ge(s_fill, 2)
            pe.wait_ge(s_meta, 32)
            seen_x = pe.alloc_register("seen_x")
            pe.reg_mov(seen_x, 0)

            def hidden(rnd, g, half, at, i):
                par, k = at // GPS, at % GPS
                if k == 0 and half == 0:
                    pe.wait_ge(s_ef[par], 16 * uses(rnd, par, i))
                pe.wait_ge(s_relu, (rnd * NG + g) * 2 + half + CREDIT)
                lo = k * GE + half * HE
                pe.matmul(ps_h[:, 0:HE], w1_sb[:], ef[:, par, lo:lo + HE],
                          start=True, stop=True).then_inc(s_h, 1)

            def weights(rnd, g, slot, tiles):
                if tiles[0] == 0:
                    pe.wait_ge(s_prod, rnd * NG + g - 1 + CREDIT)
                    pe.wait_ge(s_relu, (rnd * NG + g) * 2 + 2 + CREDIT)
                for t in tiles:
                    last = pe.matmul(w_slot(slot)[:, t * WC:(t + 1) * WC], h_sb[:, slot, t * P:(t + 1) * P],
                                     w2_sb[:], start=True, stop=True)
                if tiles[-1] == TPG - 1:
                    last.then_inc(s_w, 1)

            def window_sum(messages, one_hot):
                for t in range(TPG):
                    last = pe.matmul(win_sum, messages[:, t, :], one_hot[:, t, :],
                                     start=(t == 0), stop=(t == TPG - 1))
                return last

            for rnd in range(ROUNDS):
                if rnd > 0:
                    pe.wait_ge(s_new, len(STEPS) * rnd)
                    pe.wait_ge(s_rows, BANKS * rnd)
                hidden(rnd, 0, 0, 0, 0)
                hidden(rnd, 0, 1, 0, 0)
                hidden(rnd, 1, 0, 1, 0)
                weights(rnd, 0, 0, range(TPG))
                hidden(rnd, 1, 1, 1, 0)

                def emit(i, par, last, rnd=rnd):
                    for k in range(GPS):
                        g = (2 * i + par) * GPS + k
                        at = par * GPS + k
                        nxt, i_nxt = (at + 2) % (2 * GPS), i + (at + 2) // (2 * GPS)
                        for half in range(2):
                            if not (last and k + 2 >= GPS):
                                hidden(rnd, g + 2, half, nxt, i_nxt)
                            if not (last and k + 1 >= GPS):
                                weights(rnd, g + 1, (at + 1) % 2, (range(0, 3), range(3, TPG))[half])
                        pe.wait_ge(s_hot, rnd * NG + g + 1)
                        pe.wait_ge(s_msg, rnd * NG + g + 1)
                        pe.wait_ge(s_acc, rnd * NG + g + CREDIT + rnd)
                        window_sum(msg[:, at], hot[:, at % 2]).then_inc(s_agg, 1)
                    sub = 2 * i + par
                    more = pe.value_load(meta[0:1, bass.ds(sub * META + 2 * GPS, 1)],
                                         min_val=0, max_val=N // WIN)
                    with pe.If(more > 0):
                        for k in range(GPS):
                            n_x = pe.value_load(meta[0:1, bass.ds(sub * META + GPS + k, 1)],
                                                min_val=0, max_val=N // WIN)
                            with pe.If(n_x > 0):
                                with pe.Fori(0, n_x):
                                    pe.reg_add(seen_x, seen_x, 1)
                                    pe.wait_ge(s_hot_x, seen_x)
                                    window_sum(msg[:, par * GPS + k], hot_x).then_inc(s_agg_x, 1)

                for_subs(pe, emit)

                for c, (off, w) in enumerate(STEPS):
                    k = rnd * len(STEPS) + c
                    pe.wait_ge(s_norm, k + 1)
                    pe.wait_ge(s_new, k)
                    h = hq[:, off:off + w]
                    a = agg_q[:, c % 2, 0:w]
                    for g in range(2):
                        bank = ps_w[:, BANK * g:BANK * g + w]
                        pe.matmul(bank, gate_w[:, g, :], a, start=True, stop=False)
                        pe.matmul(bank, gate_w[:, 3 + g, :], h, start=False, stop=True)
                    pe.matmul(ps_w[:, IN_BANK:IN_BANK + w], gate_w[:, 2, :], a, start=True, stop=True)
                    pe.matmul(ps_w[:, HN_BANK:HN_BANK + w], gate_w[:, 5, :], h, start=True,
                              stop=True).then_inc(s_gate, 1)
                pe.wait_ge(s_new, len(STEPS) * (rnd + 1))
                for b in range(BANKS):
                    if b >= 2:
                        pe.wait_ge(s_rows, BANKS * rnd + b - 1)
                    for j in range(b * TR_BANK, min(RJ, (b + 1) * TR_BANK)):
                        col = TR_BANK0 + (b % 2) * BANK + (j % TR_BANK) * P
                        nodes = hq[:, :].rearrange("c (p j) -> c j p", j=RJ)[:, j, :]
                        last = pe.matmul(ps_w[0:RP, col:col + P], nodes, ident[:], start=True, stop=True)
                    last.then_inc(s_tr, 1)

        @block.vector
        def _(dve):
            links = [0]

            def link(ins):
                links[0] += 1
                ins.then_inc(s_link, 1)
                dve.wait_ge(s_link, links[0])

            dve.sem_inc(s_prod, CREDIT)
            dve.sem_inc(s_acc, CREDIT)
            dve.wait_ge(s_dst, 32)
            by_group = dst_nat[:].rearrange("s (g e) -> s g e", g=GPS)
            dve.tensor_reduce(lo_hi[:, 0, :], by_group, AX_X, ALU.min).then_inc(s_pro, 1)
            dve.tensor_reduce(lo_hi[:, 1, :], by_group, AX_X, ALU.max).then_inc(s_pro, 1)
            dve.memset(meta_w[:], 0).then_inc(s_pro, 1)
            dve.wait_ge(s_pro, 3)
            dve.tensor_tensor(span[:], lo_hi[:, 1, :], lo_hi[:, 0, :], ALU.subtract).then_inc(s_pro, 1)
            dve.tensor_copy(meta_w[:, 0:GPS], lo_hi[:, 0, :]).then_inc(s_pro, 1)
            dve.wait_ge(s_pro, 5)
            dve.tensor_scalar(meta_w[:, GPS:2 * GPS], span[:], WIN.bit_length() - 1, None,
                              ALU.logical_shift_right).then_inc(s_pro, 1)
            dve.wait_ge(s_pro, 6)
            dve.tensor_reduce(meta_w[:, 2 * GPS:2 * GPS + 1], meta_w[:, GPS:2 * GPS], AX_X,
                              ALU.max).then_inc(s_pro, 1)
            dve.wait_ge(s_const, 16 * N_CONST)
            dve.wait_ge(s_fill, 2)
            dve.wait_ge(s_hq, 16 * QUADS)
            link(dve.tensor_tensor(bias_rz[:], bias_ih[:, 0:2], bias_hh[:, 0:2], ALU.add))
            dve.wait_ge(s_meta, 32)
            seen_x = dve.alloc_register("seen_x")
            dve.reg_mov(seen_x, 0)
            start_x = dve.alloc_register("start_x")
            iota_b = win_iota[:].unsqueeze(1).to_broadcast([P, TPG, WIN])

            def products(rnd, g, at, i):
                par = at // GPS
                dve.wait_ge(s_w, rnd * NG + g + 1 + CREDIT)
                dve.wait_ge(s_xg[at], 16 * TPG * uses(rnd, par, i))
                w = w_slot(at % 2).rearrange("p (t o i) -> p t o i", t=TPG, o=C)
                xb = xg[:, at].unsqueeze(2).to_broadcast([P, TPG, C, C])
                dve.tensor_tensor(prod[:, at % 2], w, xb, ALU.mult).then_inc(s_prod, 1)

            def relative(rnd, sub, i, par):
                dve.tensor_tensor(
                    rel[:, par, :].rearrange("p (g t) -> p g t", g=GPS),
                    dst_sb[:, bass.ds(sub * TPS, TPS)].rearrange("p (g t) -> p g t", g=GPS),
                    base_all[:, bass.ds(sub * GPS, GPS)].unsqueeze(2).to_broadcast([P, GPS, TPG]),
                    ALU.subtract).then_inc(s_rel, 1)

            def one_hot(to, of):
                return dve.tensor_tensor(to, iota_b, of.unsqueeze(2).to_broadcast([P, TPG, WIN]),
                                         ALU.is_equal)

            for rnd in range(ROUNDS):
                if rnd > 0:
                    dve.wait_ge(s_zero, rnd)
                products(rnd, 0, 0, 0)

                def emit(i, par, last, rnd=rnd):
                    sub = 2 * i + par
                    relative(rnd, sub, i, par)
                    dve.wait_ge(s_rel, rnd * NSUB + sub + 1)
                    for k in range(GPS):
                        g = sub * GPS + k
                        at = par * GPS + k
                        start = dve.value_load(meta[0:1, bass.ds(sub * META + k, 1)],
                                               min_val=0, max_val=N - 1)
                        dve.wait_ge(s_agg, rnd * NG + g - 1 + CREDIT)
                        one_hot(hot[:, at % 2], rel[:, par, k * TPG:(k + 1) * TPG]).then_inc(s_hot, 1)
                        dve.wait_ge(s_prod, rnd * NG + g + 1 + CREDIT)
                        dve.tensor_reduce(msg[:, at, :, 0:C], prod[:, at % 2], AX_X, ALU.add).then_inc(s_msg, 1)
                        if not (last and k == GPS - 1):
                            dve.wait_ge(s_msg, rnd * NG + g)
                            products(rnd, g + 1, (at + 1) % (2 * GPS), i + (at + 1) // (2 * GPS))
                        dve.wait_ge(s_agg, rnd * NG + g + 1 + CREDIT)
                        dve.wait_ge(s_acc, rnd * NG + g + CREDIT + rnd)
                        window = acc[:, bass.ds(start, WIN)]
                        dve.tensor_tensor(window, window, win_sum, ALU.add).then_inc(s_acc, 1)
                    more = dve.value_load(meta[0:1, bass.ds(sub * META + 2 * GPS, 1)],
                                          min_val=0, max_val=N // WIN)
                    with dve.If(more > 0):
                        for k in range(GPS):
                            n_x = dve.value_load(meta[0:1, bass.ds(sub * META + GPS + k, 1)],
                                                 min_val=0, max_val=N // WIN)
                            with dve.If(n_x > 0):
                                start = dve.value_load(meta[0:1, bass.ds(sub * META + k, 1)],
                                                       min_val=0, max_val=N - 1)
                                dve.tensor_copy(rel_x[:], rel[:, par, k * TPG:(k + 1) * TPG])
                                dve.drain()
                                dve.reg_mov(start_x, start)
                                with dve.Fori(0, n_x):
                                    dve.tensor_scalar(rel_x[:], rel_x[:], -float(WIN), None, ALU.add)
                                    dve.drain()
                                    one_hot(hot_x[:], rel_x[:]).then_inc(s_hot_x, 1)
                                    dve.reg_add(seen_x, seen_x, 1)
                                    dve.wait_ge(s_agg_x, seen_x)
                                    dve.reg_add(start_x, start_x, WIN)
                                    at_x = dve.snap(start_x, min_val=0, max_val=N - 1)
                                    window = acc[:, bass.ds(at_x, WIN)]
                                    dve.tensor_tensor(window, window, win_sum, ALU.add)
                                    dve.drain()

                for_subs(dve, emit)
                dve.drain().then_inc(s_acc, 1)

                def mean(c):
                    off, w = STEPS[c]
                    k = rnd * len(STEPS) + c
                    dve.wait_ge(s_pack, k + 1)
                    cnt, agg = cnt_q[:, c % 2, 0:w], agg_q[:, c % 2, 0:w]
                    link(dve.tensor_scalar(cnt, cnt, 1.0, None, ALU.max))
                    link(dve.reciprocal(cnt, cnt))
                    dve.tensor_tensor(agg, agg, cnt, ALU.mult).then_inc(s_norm, 1)

                mean(0)
                for c, (off, w) in enumerate(STEPS):
                    if c + 1 < len(STEPS):
                        mean(c + 1)
                    k = rnd * len(STEPS) + c
                    r, z, t, n, h = r_q[:, 0:w], z_q[:, 0:w], t_q[:, 0:w], n_q[:, 0:w], hq[:, off:off + w]
                    dve.wait_ge(s_rz, k + 1)
                    link(dve.scalar_tensor_tensor(out=t, in0=ps_w[:, HN_BANK:HN_BANK + w], scalar=bias_hh[:, 2:3],
                                                  in1=r, op0=ALU.add, op1=ALU.mult))
                    dve.tensor_tensor(t, t, ps_w[:, IN_BANK:IN_BANK + w], ALU.add).then_inc(s_pre, 1)
                    dve.wait_ge(s_n, k + 1)
                    link(dve.tensor_tensor(t, h, n, ALU.subtract))
                    link(dve.tensor_tensor(t, t, z, ALU.mult))
                    dve.tensor_tensor(h, n, t, ALU.add).then_inc(s_new, 1)
                if rnd > 0:
                    dve.wait_ge(s_table, 16 * rnd)
                for b in range(BANKS):
                    lo, hi = b * TR_BANK, min(RJ, (b + 1) * TR_BANK)
                    dve.wait_ge(s_tr, BANKS * rnd + b + 1)
                    at = TR_BANK0 + (b % 2) * BANK
                    bank = ps_w[0:RP, at:at + (hi - lo) * P]
                    dve.tensor_copy(rows[:, :, lo:hi, :],
                                    bank.rearrange("p (j q c) -> p q j c", q=QUADS, c=QS)[:, :, :, 0:C]
                                    ).then_inc(s_rows, 1)

            dve.wait_ge(s_rows, BANKS * ROUNDS)
            y = rows[:].rearrange("p q j c -> p (q j) c")
            xr = xrows[:].rearrange("p q j c -> p (q j) c")
            wide = [RP, QUADS * RJ, C]
            link(dve.tensor_tensor(y, y, xr, ALU.add))
            link(dve.tensor_reduce(stat[:, 0, :], y, AX_X, ALU.add))
            link(dve.tensor_scalar(stat[:, 0, :], stat[:, 0, :], 1.0 / C, None, ALU.mult))
            link(dve.tensor_tensor(cent[:], y, stat[:, 0, :].unsqueeze(2).to_broadcast(wide), ALU.subtract))
            link(dve.tensor_tensor(y, cent[:], cent[:], ALU.mult))
            dve.tensor_reduce(stat[:, 1, :], y, AX_X, ALU.add).then_inc(s_ln, 1)
            dve.wait_ge(s_sd, 1)
            link(dve.reciprocal(stat[:, 3, :], stat[:, 2, :]))
            dve.tensor_tensor(y, cent[:], stat[:, 3, :].unsqueeze(2).to_broadcast(wide),
                              ALU.mult).then_inc(s_y, 1)


def kernel(x, src, dst, edge_attr_13, L0_gnn_fnet_w1, L0_gnn_fnet_b1, L0_gnn_fnet_w2, L0_gnn_fnet_b2,
           L0_gnn_gru_w_ih, L0_gnn_gru_w_hh, L0_gnn_gru_b_ih, L0_gnn_gru_b_hh):
    import numpy as np
    import concourse.bacc as bacc
    from concourse.bass_utils import run_bass_kernel_spmd

    def lay(a):
        return np.ascontiguousarray(a)

    N, C = x.shape
    E, FD = edge_attr_13.shape
    HID = L0_gnn_fnet_w1.shape[1]
    TPS = TPG * GPS

    def tiles(a):
        return np.asarray(a).reshape(-1, TPS, P).transpose(0, 2, 1)

    arrays = {
        "x": lay(x),
        "x_t": lay(np.asarray(x).T),
        "src_tiles": lay(tiles(src).reshape(-1, TPS)),
        "dst": lay(dst),
        "dst_tiles": lay(tiles(dst).transpose(1, 0, 2).reshape(P, -1)),
        "ef_t": lay(np.asarray(edge_attr_13).T),
        "w1": lay(L0_gnn_fnet_w1),
        "b1": lay(np.asarray(L0_gnn_fnet_b1).reshape(HID, 1)),
        "w2_oi": lay(np.asarray(L0_gnn_fnet_w2).reshape(HID, C, C).transpose(0, 2, 1).reshape(HID, C * C)),
        "b2_oi": lay(np.asarray(L0_gnn_fnet_b2).reshape(1, C, C).transpose(0, 2, 1).reshape(1, C * C)),
        "w_ih_t": lay(np.asarray(L0_gnn_gru_w_ih).T),
        "w_hh_t": lay(np.asarray(L0_gnn_gru_w_hh).T),
        "b_ih_g": lay(np.asarray(L0_gnn_gru_b_ih).reshape(3, C).T),
        "b_hh_g": lay(np.asarray(L0_gnn_gru_b_hh).reshape(3, C).T),
    }
    nc = bacc.Bacc("TRN2", target_bir_lowering=False, num_devices=1)
    aps = {k: nc.dram_tensor("in_" + k, a.shape, mybir.dt.from_np(a.dtype), kind="ExternalInput").ap()
           for k, a in arrays.items()}
    out = nc.dram_tensor("out_0", (N, C), F32, kind="ExternalOutput").ap()
    gnn_program(nc, out=out, **aps)
    r = run_bass_kernel_spmd(nc, [{"in_" + k: a for k, a in arrays.items()}], core_ids=[0])
    return r.results[0]["out_0"]
```

```python
from contextlib import ExitStack

import concourse.bass as bass
from concourse import mybir

P = 128
BANK = 512
F32 = mybir.dt.float32
I32 = mybir.dt.int32
U32 = mybir.dt.uint32
ALU = mybir.AluOpType
ACT = mybir.ActivationFunctionType
AX_X = mybir.AxisListType.X

TPG = 5
GPS = 5
WIN = 64
QUADS = 4
QS = 32
CNT = 32
CREDIT = 16
META = 12
LN_EPS = 1e-5


def gnn_program(nc, x, x_t, src_tiles, dst, dst_tiles, ef_t, w1, b1, w2_oi, b2_oi,
                gate_w_t, gate_b, out):
    N, C = x.shape
    FD, E = ef_t.shape
    HID = w1.shape[1]
    HA = HID + 1
    WC = C * C
    GE = TPG * P
    HE = GE // 2
    SE = GPS * GE
    TPS = TPG * GPS
    NSUB = E // SE
    NG = NSUB * GPS
    PAIRS, TAIL = NSUB // 2, NSUB % 2
    Q = N // QUADS
    RP = 125
    RJ = Q // RP
    ROUNDS = 2
    JW = BANK // P
    STEPS = [(RP * j, RP * min(JW, RJ - j), j, min(JW, RJ - j)) for j in range(0, RJ, JW)]
    GW = RP * JW
    NS = len(STEPS)
    AGG_SLOTS = 3
    assert TAIL == 1
    assert E % SE == 0 and NSUB <= P and N % QUADS == 0 and Q % RP == 0 and C == 16

    def uses(rnd, par, i):
        per_round = PAIRS + (TAIL if par == 0 else 0)
        return i + (rnd * per_round + 1)

    table2 = nc.dram_tensor("h_rows", [N, C], F32, kind="Internal").ap()
    meta_d = nc.dram_tensor("meta_d", [NSUB, META], I32, kind="Internal").ap()
    base_d = nc.dram_tensor("base_d", [NSUB, GPS], F32, kind="Internal").ap()

    with ExitStack() as ctx:
        def sb(name, shape, dt=F32):
            return ctx.enter_context(nc.sbuf_tensor(name, shape, dt))

        def ps(name, shape):
            return ctx.enter_context(nc.psum_tensor(name, shape, F32))

        def sem(name):
            return ctx.enter_context(nc.semaphore(name))

        w1_sb = sb("w1_sb", [P, P])
        b1_sb = sb("b1_sb", [P, 1])
        w2_sb = sb("w2_sb", [P, WC])
        gate_w = sb("gate_w", [P, 6, P])
        bias = sb("bias", [P, 6])
        bias_rz = sb("bias_rz", [P, 2])
        ident = sb("ident", [P, P])
        win_iota = sb("win_iota", [P, WIN])
        eps = sb("eps", [P, 1])
        dst_nat = sb("dst_nat", [P, SE], I32)
        dst_sb = sb("dst_sb", [P, NSUB * TPS], I32)
        base_all = sb("base_all", [P, NG])
        lo_hi = sb("lo_hi", [NSUB, 2, GPS])
        span = sb("span", [NSUB, GPS], I32)
        meta_w = sb("meta_w", [NSUB, META], I32)
        meta = sb("meta", [1, NSUB * META], I32)
        idx = sb("idx", [P, 2, TPS], I32)
        ef = sb("ef", [P, 2, SE])
        h_sb = sb("h_sb", [P, 2, GE])
        xg = sb("xg", [P, 2 * GPS, TPG, C])
        rel = sb("rel", [P, 2, TPS])
        prod = sb("prod", [P, 2, TPG, C, C])
        hot = sb("hot", [P, 2, TPG, WIN])
        msg = sb("msg", [P, 2 * GPS, TPG, CNT + C])
        rel_x = sb("rel_x", [P, TPG])
        hot_x = sb("hot_x", [P, TPG, WIN])
        acc = sb("acc", [CNT + C, N + WIN])
        hq = sb("hq", [P, Q])
        agg_q = sb("agg_q", [P, AGG_SLOTS, GW])
        inv_q = dst_nat[:, 0:Q].bitcast(F32)
        r_q = sb("r_q", [P, 2, GW])
        z_q = sb("z_q", [P, 2, GW])
        t_q = sb("t_q", [P, 2, GW])
        n_q = sb("n_q", [P, 2, GW])
        rows = sb("rows", [RP, QUADS, RJ, C])
        xrows = sb("xrows", [RP, QUADS, RJ, C])
        cent = sb("cent", [RP, QUADS * RJ, C])
        stat = sb("stat", [RP, 4, QUADS * RJ])

        ps_w = ps("ps_w", [P, 6 * BANK])
        ps_h = ps("ps_h", [P, BANK])
        ps_a = ps("ps_a", [P, BANK])
        win_sum = ps_a[0:CNT + C, 0:WIN]
        R_BANK, Z_BANK, IN_BANK, HN_BANK, TR_BANK0 = (BANK * b for b in range(5))

        def w_slot(s):
            return ps_w[:, s * 3 * BANK:s * 3 * BANK + TPG * WC]

        s_net = sem("s_net")
        s_gru = sem("s_gru")
        s_dst = sem("s_dst")
        s_xrows = sem("s_xrows")
        s_fill = sem("s_fill")
        s_ident = sem("s_ident")
        s_meta_w = sem("s_meta_w")
        s_meta = sem("s_meta")
        s_pro = sem("s_pro")
        s_ef = [sem(f"s_ef{p}") for p in range(2)]
        s_idx = [sem(f"s_idx{p}") for p in range(2)]
        s_xg = [sem(f"s_xg{k}") for k in range(2 * GPS)]
        s_h = sem("s_h")
        s_relu = sem("s_relu")
        s_w = sem("s_w")
        s_rel = sem("s_rel")
        s_prod = sem("s_prod")
        s_hot = sem("s_hot")
        s_msg = sem("s_msg")
        s_agg = sem("s_agg")
        s_acc = sem("s_acc")
        s_hot_x = sem("s_hot_x")
        s_agg_x = sem("s_agg_x")
        s_pack = sem("s_pack")
        s_cnt = sem("s_cnt")
        s_norm = sem("s_norm")
        s_gate = sem("s_gate")
        s_rz = sem("s_rz")
        s_pre = sem("s_pre")
        s_n = sem("s_n")
        s_new = sem("s_new")
        s_link = sem("s_link")
        s_tr = sem("s_tr")
        s_rows = sem("s_rows")
        s_table = sem("s_table")
        s_zero = sem("s_zero")
        s_ln = sem("s_ln")
        s_sd = sem("s_sd")
        s_y = sem("s_y")
        s_out = sem("s_out")

        NET_LOADS = 4
        GRU_LOADS = 3 * QUADS
        FILLED_EF, FILLED_NET, FILLED = 1, 2, 3

        def node_rows(table, c):
            off, w, _, jn = STEPS[c]
            return table.rearrange("(q n) c -> q n c", q=QUADS)[:, off:off + w, :].rearrange(
                "q (p j) c -> p q (j c)", j=jn)

        def step_rows(t, c):
            _, _, j, jn = STEPS[c]
            return t[:, :, j:j + jn, :]

        def step_bank(c):
            jn = STEPS[c][3]
            lo = TR_BANK0 + (c % 2) * BANK
            return ps_w[0:RP, lo:lo + jn * P].rearrange(
                "p (j q c) -> p q j c", q=QUADS, c=QS)[:, :, :, 0:C]

        block = ctx.enter_context(nc.Block())

        def for_subs(eng, emit):
            if PAIRS:
                with eng.Fori(0, PAIRS) as i:
                    emit(i, 0, False)
                    emit(i, 1, TAIL == 0)
            if TAIL:
                emit(PAIRS, 0, True)

        @block.sync
        def _(sp):
            for rnd in range(ROUNDS):
                def emit(i, par, last, rnd=rnd):
                    sub = 2 * i + par
                    done = rnd * NG + (sub - 1) * GPS
                    sp.wait_ge(s_prod, done + CREDIT)
                    sp.dma_start(idx[:, par, :], src_tiles[bass.ds(sub * P, P), :]).then_inc(s_idx[par], 16)
                    sp.wait_ge(s_fill, FILLED_EF)
                    sp.wait_ge(s_h, done * 2 + CREDIT)
                    sp.dma_start(ef[0:FD, par, :], ef_t[:, bass.ds(sub * SE, SE)]).then_inc(s_ef[par], 16)

                for_subs(sp, emit)
                if rnd < ROUNDS - 1:
                    for c in range(NS):
                        sp.wait_ge(s_rows, NS * rnd + c + 1)
                        sp.dma_start(node_rows(table2, c), step_rows(rows, c)).then_inc(s_table, 16)
                    for c in range(NS):
                        sp.dma_start(step_rows(xrows, c), node_rows(x, c)).then_inc(s_xrows, 16)
            sp.wait_ge(s_y, 1)
            for c in range(NS):
                sp.dma_start(node_rows(out, c), step_rows(rows, c)).then_inc(s_out, 16)
            sp.wait_ge(s_out, 16 * NS)
            sp.wait_ge(s_table, 16 * NS * (ROUNDS - 1))

        @block.gpsimd
        def _(pool):
            pool.memset(ident[:], 0.0)
            pool.iota(win_iota[:], [[1, WIN]], base=0, channel_multiplier=0,
                      allow_small_or_imprecise_dtypes=True)
            pool.drain()
            pool.affine_select(out=ident[:], in_=ident[:], compare_op=ALU.not_equal, fill=1.0, base=0,
                               pattern=[[-1, P]], channel_multiplier=1).then_inc(s_ident, 1)

            for rnd in range(ROUNDS):
                table = x if rnd == 0 else table2
                if rnd > 0:
                    pool.wait_ge(s_table, 16 * NS * rnd)

                def emit(i, par, last, rnd=rnd, table=table):
                    pool.wait_ge(s_idx[par], 16 * uses(rnd, par, i))
                    for k in range(GPS):
                        g = (2 * i + par) * GPS + k
                        pool.wait_ge(s_prod, rnd * NG + g - 2 * GPS + 1 + CREDIT)
                        pool.nop(nofuse=True)
                        for t in range(TPG):
                            pool.indirect_dma_start(
                                out=xg[:, par * GPS + k, t, :], out_offset=None, in_=table,
                                in_offset=bass.IndirectOffsetOnAxis(
                                    ap=idx[:, par, k * TPG + t:k * TPG + t + 1].bitcast(U32), axis=0),
                            ).then_inc(s_xg[par * GPS + k], 16)

                for_subs(pool, emit)
                if rnd < ROUNDS - 1:
                    pool.wait_ge(s_norm, NS * (rnd + 1))
                    pool.memset(acc[:], 0.0).then_inc(s_zero, 1)

        @block.scalar
        def _(act):
            act.sem_inc(s_relu, CREDIT)
            act.dma_start(dst_nat[0:NSUB, :], dst.rearrange("(s e) -> s e", s=NSUB)).then_inc(s_dst, 16)
            act.dma_start(dst_sb[:], dst_tiles).then_inc(s_dst, 16)
            act.wait_ge(s_fill, FILLED_NET)
            act.dma_start(w1_sb[0:FD, 0:HID], w1).then_inc(s_net, 16)
            act.dma_start(b1_sb[0:HID, :], b1).then_inc(s_net, 16)
            act.dma_start(w2_sb[0:HID, :], w2_oi).then_inc(s_net, 16)
            act.dma_start(w2_sb[HID:HA, :], b2_oi).then_inc(s_net, 16)
            act.wait_ge(s_pro, 7)
            act.dma_start(meta_d, meta_w[:]).then_inc(s_meta_w, 16)
            act.dma_start(base_d, lo_hi[:, 0, :]).then_inc(s_meta_w, 16)
            act.wait_ge(s_meta_w, 32)
            act.dma_start(meta[:], meta_d.rearrange("s m -> (s m)").unsqueeze(0)).then_inc(s_meta, 16)
            act.dma_start(base_all[:], base_d.rearrange("s g -> (s g)").unsqueeze(0)
                          .to_broadcast([P, NG])).then_inc(s_meta, 16)
            act.wait_ge(s_fill, FILLED)
            for q in range(QUADS):
                lo = QS * q
                act.dma_start(gate_w[lo:lo + C, :, lo:lo + C], gate_w_t).then_inc(s_gru, 16)
                act.dma_start(bias[lo:lo + C, :], gate_b).then_inc(s_gru, 16)
                act.dma_start(hq[lo:lo + C, :], x_t[:, q * Q:(q + 1) * Q]).then_inc(s_gru, 16)
            act.wait_ge(s_net, 16 * NET_LOADS)

            def pack(rnd, c):
                off, w, _, _ = STEPS[c]
                if c >= AGG_SLOTS:
                    act.wait_ge(s_gate, rnd * NS + c - AGG_SLOTS + 1)
                for q in range(QUADS):
                    last = act.copy(agg_q[QS * q:QS * q + C, c % AGG_SLOTS, 0:w],
                                    acc[0:C, q * Q + off:q * Q + off + w])
                last.then_inc(s_pack, 1)
                if rnd == 0:
                    for q in range(0, QUADS, 2):
                        last = act.copy(inv_q[QS * q:QS * q + C, off:off + w],
                                        acc[CNT:CNT + C, q * Q + off:q * Q + off + w])
                    last.then_inc(s_cnt, 1)

            def to_rows(rnd, c):
                act.wait_ge(s_tr, rnd * NS + c + 1)
                act.copy(step_rows(rows, c), step_bank(c)).then_inc(s_rows, 1)

            for rnd in range(ROUNDS):
                def emit(i, par, last, rnd=rnd):
                    for k in range(GPS):
                        g = (2 * i + par) * GPS + k
                        act.wait_ge(s_w, rnd * NG + g - 1 + CREDIT)
                        for half in range(2):
                            act.wait_ge(s_h, (rnd * NG + g) * 2 + half + 1 + CREDIT)
                            act.activation(h_sb[:, (par * GPS + k) % 2, half * HE:(half + 1) * HE],
                                           ps_h[:, 0:HE], ACT.Relu,
                                           bias=b1_sb[:, 0:1]).then_inc(s_relu, 1)

                for_subs(act, emit)
                act.wait_ge(s_acc, NG * (rnd + 1) + CREDIT + rnd + 1)
                for c in range(AGG_SLOTS):
                    pack(rnd, c)
                for c, (off, w, _, _) in enumerate(STEPS):
                    k = rnd * NS + c
                    act.wait_ge(s_gate, k + 1)
                    act.wait_ge(s_new, k - 1 if c else 0)
                    act.activation(r_q[:, c % 2, 0:w], ps_w[:, R_BANK:R_BANK + w], ACT.Sigmoid,
                                   bias=bias_rz[:, 0:1])
                    act.activation(z_q[:, c % 2, 0:w], ps_w[:, Z_BANK:Z_BANK + w], ACT.Sigmoid,
                                   bias=bias_rz[:, 1:2]).then_inc(s_rz, 1)
                    if c + AGG_SLOTS < NS:
                        pack(rnd, c + AGG_SLOTS)
                    act.wait_ge(s_pre, k + 1)
                    act.activation(n_q[:, c % 2, 0:w], t_q[:, c % 2, 0:w], ACT.Tanh,
                                   bias=bias[:, 2:3]).then_inc(s_n, 1)
                    if c > 0 and rnd < ROUNDS - 1:
                        to_rows(rnd, c - 1)
                if rnd < ROUNDS - 1:
                    to_rows(rnd, NS - 1)
            act.wait_ge(s_ln, 1)
            act.activation(stat[:, 2, :], stat[:, 1, :], ACT.Sqrt, bias=eps[0:RP, :],
                           scale=1.0 / C).then_inc(s_sd, 1)

        @block.tensor
        def _(pe):
            pe.sem_inc(s_h, CREDIT)
            pe.sem_inc(s_w, CREDIT)
            pe.sem_inc(s_agg, CREDIT)
            pe.wait_ge(s_net, 16 * NET_LOADS)
            pe.wait_ge(s_meta, 32)
            seen_x = pe.alloc_register("seen_x")
            pe.reg_mov(seen_x, 0)

            def hidden(rnd, g, half, at, i):
                par, k = at // GPS, at % GPS
                if k == 0 and half == 0:
                    pe.wait_ge(s_ef[par], 16 * uses(rnd, par, i))
                pe.wait_ge(s_relu, (rnd * NG + g) * 2 + half + CREDIT)
                lo = k * GE + half * HE
                pe.matmul(ps_h[:, 0:HE], w1_sb[:], ef[:, par, lo:lo + HE],
                          start=True, stop=True).then_inc(s_h, 1)

            def weights(rnd, g, slot, tiles):
                if tiles[0] == 0:
                    pe.wait_ge(s_prod, rnd * NG + g - 1 + CREDIT)
                    pe.wait_ge(s_relu, (rnd * NG + g) * 2 + 2 + CREDIT)
                for t in tiles:
                    last = pe.matmul(w_slot(slot)[:, t * WC:(t + 1) * WC], h_sb[:, slot, t * P:(t + 1) * P],
                                     w2_sb[:], start=True, stop=True)
                if tiles[-1] == TPG - 1:
                    last.then_inc(s_w, 1)

            def window_sum(messages, one_hot):
                for t in range(TPG):
                    last = pe.matmul(win_sum, messages[:, t, :], one_hot[:, t, :],
                                     start=(t == 0), stop=(t == TPG - 1))
                return last

            for rnd in range(ROUNDS):
                if rnd > 0:
                    pe.wait_ge(s_rows, NS * rnd)
                hidden(rnd, 0, 0, 0, 0)
                hidden(rnd, 0, 1, 0, 0)
                hidden(rnd, 1, 0, 1, 0)
                weights(rnd, 0, 0, range(TPG))
                hidden(rnd, 1, 1, 1, 0)

                def emit(i, par, last, rnd=rnd):
                    for k in range(GPS):
                        g = (2 * i + par) * GPS + k
                        at = par * GPS + k
                        nxt, i_nxt = (at + 2) % (2 * GPS), i + (at + 2) // (2 * GPS)
                        for half in range(2):
                            if not (last and k + 2 >= GPS):
                                hidden(rnd, g + 2, half, nxt, i_nxt)
                            if not (last and k + 1 >= GPS):
                                weights(rnd, g + 1, (at + 1) % 2, (range(0, 3), range(3, TPG))[half])
                        pe.wait_ge(s_hot, rnd * NG + g + 1)
                        pe.wait_ge(s_msg, rnd * NG + g + 1)
                        pe.wait_ge(s_acc, rnd * NG + g + CREDIT + rnd)
                        window_sum(msg[:, at], hot[:, at % 2]).then_inc(s_agg, 1)
                    sub = 2 * i + par
                    more = pe.value_load(meta[0:1, bass.ds(sub * META + 2 * GPS, 1)],
                                         min_val=0, max_val=N // WIN)
                    with pe.If(more > 0):
                        for k in range(GPS):
                            n_x = pe.value_load(meta[0:1, bass.ds(sub * META + GPS + k, 1)],
                                                min_val=0, max_val=N // WIN)
                            with pe.If(n_x > 0):
                                with pe.Fori(0, n_x):
                                    pe.reg_add(seen_x, seen_x, 1)
                                    pe.wait_ge(s_hot_x, seen_x)
                                    window_sum(msg[:, par * GPS + k], hot_x).then_inc(s_agg_x, 1)

                for_subs(pe, emit)

                pe.wait_ge(s_gru, 16 * GRU_LOADS)
                pe.wait_ge(s_ident, 1)

                def transposes(c):
                    off, w, _, jn = STEPS[c]
                    pe.wait_ge(s_new, rnd * NS + c + 1)
                    if c >= 2:
                        pe.wait_ge(s_rows, rnd * NS + c - 1)
                    for j in range(jn):
                        col = TR_BANK0 + (c % 2) * BANK + j * P
                        nodes = hq[:, off:off + w].rearrange("c (p j) -> c j p", j=jn)[:, j, :]
                        last = pe.matmul(ps_w[0:RP, col:col + P], nodes, ident[:], start=True, stop=True)
                    last.then_inc(s_tr, 1)

                for c, (off, w, _, _) in enumerate(STEPS):
                    k = rnd * NS + c
                    pe.wait_ge(s_norm, k + 1)
                    pe.wait_ge(s_rz, k)
                    h = hq[:, off:off + w]
                    a = agg_q[:, c % AGG_SLOTS, 0:w]
                    for g, lo in enumerate((R_BANK, Z_BANK)):
                        pe.matmul(ps_w[:, lo:lo + w], gate_w[:, g, :], a, start=True, stop=False)
                        pe.matmul(ps_w[:, lo:lo + w], gate_w[:, 3 + g, :], h, start=False, stop=True)
                    pe.wait_ge(s_pre, k)
                    pe.matmul(ps_w[:, IN_BANK:IN_BANK + w], gate_w[:, 2, :], a, start=True, stop=True)
                    pe.matmul(ps_w[:, HN_BANK:HN_BANK + w], gate_w[:, 5, :], h, start=True,
                              stop=True).then_inc(s_gate, 1)
                    if c > 0:
                        transposes(c - 1)
                transposes(NS - 1)

        @block.vector
        def _(dve):
            links = [0]

            def link(ins):
                links[0] += 1
                ins.then_inc(s_link, 1)
                dve.wait_ge(s_link, links[0])

            dve.sem_inc(s_prod, CREDIT)
            dve.sem_inc(s_acc, CREDIT)
            dve.memset(ef[:], 0.0)
            dve.drain().then_inc(s_fill, 1)
            for t in (w1_sb, w2_sb, b1_sb):
                dve.memset(t[:], 0.0)
            dve.drain()
            dve.memset(b1_sb[HID:HA, :], 1.0)
            dve.drain().then_inc(s_fill, 1)
            dve.wait_ge(s_dst, 32)
            by_group = dst_nat[0:NSUB, :].rearrange("s (g e) -> s g e", g=GPS)
            dve.tensor_reduce(lo_hi[:, 0, :], by_group, AX_X, ALU.min).then_inc(s_pro, 1)
            dve.tensor_reduce(lo_hi[:, 1, :], by_group, AX_X, ALU.max).then_inc(s_pro, 1)
            dve.memset(meta_w[:], 0).then_inc(s_pro, 1)
            dve.wait_ge(s_pro, 3)
            dve.tensor_tensor(span[:], lo_hi[:, 1, :], lo_hi[:, 0, :], ALU.subtract).then_inc(s_pro, 1)
            dve.tensor_copy(meta_w[:, 0:GPS], lo_hi[:, 0, :]).then_inc(s_pro, 1)
            dve.wait_ge(s_pro, 5)
            dve.tensor_scalar(meta_w[:, GPS:2 * GPS], span[:], WIN.bit_length() - 1, None,
                              ALU.logical_shift_right).then_inc(s_pro, 1)
            dve.wait_ge(s_pro, 6)
            dve.tensor_reduce(meta_w[:, 2 * GPS:2 * GPS + 1], meta_w[:, GPS:2 * GPS], AX_X,
                              ALU.max).then_inc(s_pro, 1)
            for t, v in ((gate_w, 0.0), (bias, 0.0), (hq, 0.0), (eps, LN_EPS), (acc, 0.0), (msg, 1.0),
                         (agg_q, 0.0)):
                dve.memset(t[:], v)
            dve.memset(inv_q, 1.0)
            dve.drain().then_inc(s_fill, 1)
            dve.wait_ge(s_ident, 1)
            dve.wait_ge(s_meta, 32)
            seen_x = dve.alloc_register("seen_x")
            dve.reg_mov(seen_x, 0)
            start_x = dve.alloc_register("start_x")
            iota_b = win_iota[:].unsqueeze(1).to_broadcast([P, TPG, WIN])

            def products(rnd, g, at, i):
                par = at // GPS
                dve.wait_ge(s_w, rnd * NG + g + 1 + CREDIT)
                dve.wait_ge(s_xg[at], 16 * TPG * uses(rnd, par, i))
                w = w_slot(at % 2).rearrange("p (t o i) -> p t o i", t=TPG, o=C)
                xb = xg[:, at].unsqueeze(2).to_broadcast([P, TPG, C, C])
                dve.tensor_tensor(prod[:, at % 2], w, xb, ALU.mult).then_inc(s_prod, 1)

            def relative(rnd, sub, i, par):
                dve.tensor_tensor(
                    rel[:, par, :].rearrange("p (g t) -> p g t", g=GPS),
                    dst_sb[:, bass.ds(sub * TPS, TPS)].rearrange("p (g t) -> p g t", g=GPS),
                    base_all[:, bass.ds(sub * GPS, GPS)].unsqueeze(2).to_broadcast([P, GPS, TPG]),
                    ALU.subtract).then_inc(s_rel, 1)

            def one_hot(to, of):
                return dve.tensor_tensor(to, iota_b, of.unsqueeze(2).to_broadcast([P, TPG, WIN]),
                                         ALU.is_equal)

            for rnd in range(ROUNDS):
                if rnd > 0:
                    dve.wait_ge(s_zero, rnd)
                products(rnd, 0, 0, 0)

                def emit(i, par, last, rnd=rnd):
                    sub = 2 * i + par
                    relative(rnd, sub, i, par)
                    dve.wait_ge(s_rel, rnd * NSUB + sub + 1)
                    for k in range(GPS):
                        g = sub * GPS + k
                        at = par * GPS + k
                        start = dve.value_load(meta[0:1, bass.ds(sub * META + k, 1)],
                                               min_val=0, max_val=N - 1)
                        dve.wait_ge(s_agg, rnd * NG + g - 1 + CREDIT)
                        one_hot(hot[:, at % 2], rel[:, par, k * TPG:(k + 1) * TPG]).then_inc(s_hot, 1)
                        dve.wait_ge(s_prod, rnd * NG + g + 1 + CREDIT)
                        dve.tensor_reduce(msg[:, at, :, 0:C], prod[:, at % 2], AX_X, ALU.add).then_inc(s_msg, 1)
                        if not (last and k == GPS - 1):
                            dve.wait_ge(s_msg, rnd * NG + g)
                            products(rnd, g + 1, (at + 1) % (2 * GPS), i + (at + 1) // (2 * GPS))
                        dve.wait_ge(s_agg, rnd * NG + g + 1 + CREDIT)
                        dve.wait_ge(s_acc, rnd * NG + g + CREDIT + rnd)
                        window = acc[:, bass.ds(start, WIN)]
                        dve.tensor_tensor(window, window, win_sum, ALU.add).then_inc(s_acc, 1)
                    more = dve.value_load(meta[0:1, bass.ds(sub * META + 2 * GPS, 1)],
                                          min_val=0, max_val=N // WIN)
                    with dve.If(more > 0):
                        for k in range(GPS):
                            n_x = dve.value_load(meta[0:1, bass.ds(sub * META + GPS + k, 1)],
                                                 min_val=0, max_val=N // WIN)
                            with dve.If(n_x > 0):
                                start = dve.value_load(meta[0:1, bass.ds(sub * META + k, 1)],
                                                       min_val=0, max_val=N - 1)
                                dve.tensor_copy(rel_x[:], rel[:, par, k * TPG:(k + 1) * TPG])
                                dve.drain()
                                dve.reg_mov(start_x, start)
                                with dve.Fori(0, n_x):
                                    dve.tensor_scalar(rel_x[:], rel_x[:], -float(WIN), None, ALU.add)
                                    dve.drain()
                                    one_hot(hot_x[:], rel_x[:]).then_inc(s_hot_x, 1)
                                    dve.reg_add(seen_x, seen_x, 1)
                                    dve.wait_ge(s_agg_x, seen_x)
                                    dve.reg_add(start_x, start_x, WIN)
                                    at_x = dve.snap(start_x, min_val=0, max_val=N - 1)
                                    window = acc[:, bass.ds(at_x, WIN)]
                                    dve.tensor_tensor(window, window, win_sum, ALU.add)
                                    dve.drain()

                for_subs(dve, emit)
                dve.drain().then_inc(s_acc, 1)

                def mean(c):
                    off, w, _, _ = STEPS[c]
                    inv = inv_q[:, off:off + w]
                    if rnd == 0:
                        for q in range(1, QUADS, 2):
                            last = dve.tensor_copy(inv_q[QS * q:QS * q + C, off:off + w],
                                                   acc[CNT:CNT + C, q * Q + off:q * Q + off + w])
                        dve.wait_ge(s_cnt, c + 1)
                        link(last)
                        link(dve.tensor_scalar(inv, inv, 1.0, None, ALU.max))
                        link(dve.reciprocal(inv, inv))
                    dve.wait_ge(s_pack, rnd * NS + c + 1)
                    agg = agg_q[:, c % AGG_SLOTS, 0:w]
                    dve.tensor_tensor(agg, agg, inv, ALU.mult).then_inc(s_norm, 1)

                def before_n(c):
                    w = STEPS[c][1]
                    r, t = r_q[:, c % 2, 0:w], t_q[:, c % 2, 0:w]
                    dve.wait_ge(s_rz, rnd * NS + c + 1)
                    link(dve.scalar_tensor_tensor(out=t, in0=ps_w[:, HN_BANK:HN_BANK + w],
                                                  scalar=bias[:, 5:6], in1=r, op0=ALU.add, op1=ALU.mult))
                    dve.tensor_tensor(t, t, ps_w[:, IN_BANK:IN_BANK + w], ALU.add).then_inc(s_pre, 1)

                def new_h(c):
                    off, w, _, _ = STEPS[c]
                    z, t, n, h = z_q[:, c % 2, 0:w], t_q[:, c % 2, 0:w], n_q[:, c % 2, 0:w], hq[:, off:off + w]
                    dve.wait_ge(s_n, rnd * NS + c + 1)
                    link(dve.tensor_tensor(t, h, n, ALU.subtract))
                    link(dve.tensor_tensor(t, t, z, ALU.mult))
                    dve.tensor_tensor(h, n, t, ALU.add).then_inc(s_new, 1)

                def residual(c):
                    _, _, j, jn = STEPS[c]
                    dve.wait_ge(s_tr, rnd * NS + c + 1)
                    dve.tensor_tensor(step_rows(rows, c), step_bank(c), step_rows(xrows, c),
                                      ALU.add).then_inc(s_rows, 1)

                if rnd == 0:
                    dve.wait_ge(s_gru, 16 * GRU_LOADS)
                    link(dve.tensor_tensor(bias_rz[:], bias[:, 0:2], bias[:, 3:5], ALU.add))
                if rnd == ROUNDS - 1:
                    dve.wait_ge(s_xrows, 16 * NS)
                    dve.wait_ge(s_table, 16 * NS * rnd)
                mean(0)
                mean(1)
                for c in range(NS):
                    before_n(c)
                    if c + 2 < NS:
                        mean(c + 2)
                    new_h(c)
                    if c > 0 and rnd == ROUNDS - 1:
                        residual(c - 1)
                if rnd == ROUNDS - 1:
                    residual(NS - 1)

            dve.wait_ge(s_rows, NS * ROUNDS)
            y = rows[:].rearrange("p q j c -> p (q j) c")
            wide = [RP, QUADS * RJ, C]
            link(dve.tensor_reduce(stat[:, 0, :], y, AX_X, ALU.add))
            link(dve.tensor_scalar(stat[:, 0, :], stat[:, 0, :], 1.0 / C, None, ALU.mult))
            link(dve.tensor_tensor(cent[:], y, stat[:, 0, :].unsqueeze(2).to_broadcast(wide), ALU.subtract))
            link(dve.tensor_tensor(y, cent[:], cent[:], ALU.mult))
            dve.tensor_reduce(stat[:, 1, :], y, AX_X, ALU.add).then_inc(s_ln, 1)
            dve.wait_ge(s_sd, 1)
            link(dve.reciprocal(stat[:, 3, :], stat[:, 2, :]))
            dve.tensor_tensor(y, cent[:], stat[:, 3, :].unsqueeze(2).to_broadcast(wide),
                              ALU.mult).then_inc(s_y, 1)


def kernel(x, src, dst, edge_attr_13, L0_gnn_fnet_w1, L0_gnn_fnet_b1, L0_gnn_fnet_w2, L0_gnn_fnet_b2,
           L0_gnn_gru_w_ih, L0_gnn_gru_w_hh, L0_gnn_gru_b_ih, L0_gnn_gru_b_hh):
    import numpy as np
    import concourse.bacc as bacc
    from concourse.bass_utils import run_bass_kernel_spmd

    def lay(a):
        return np.ascontiguousarray(a)

    N, C = x.shape
    E, FD = edge_attr_13.shape
    HID = L0_gnn_fnet_w1.shape[1]
    TPS = TPG * GPS

    def tiles(a):
        return np.asarray(a).reshape(-1, TPS, P).transpose(0, 2, 1)

    arrays = {
        "x": lay(x),
        "x_t": lay(np.asarray(x).T),
        "src_tiles": lay(tiles(src).reshape(-1, TPS)),
        "dst": lay(dst),
        "dst_tiles": lay(tiles(dst).transpose(1, 0, 2).reshape(P, -1)),
        "ef_t": lay(np.asarray(edge_attr_13).T),
        "w1": lay(L0_gnn_fnet_w1),
        "b1": lay(np.asarray(L0_gnn_fnet_b1).reshape(HID, 1)),
        "w2_oi": lay(np.asarray(L0_gnn_fnet_w2).reshape(HID, C, C).transpose(0, 2, 1).reshape(HID, C * C)),
        "b2_oi": lay(np.asarray(L0_gnn_fnet_b2).reshape(1, C, C).transpose(0, 2, 1).reshape(1, C * C)),
        "gate_w_t": lay(np.concatenate([np.asarray(w).reshape(3, C, C) for w in
                                        (L0_gnn_gru_w_ih, L0_gnn_gru_w_hh)]).transpose(2, 0, 1)),
        "gate_b": lay(np.concatenate([np.asarray(b).reshape(3, C) for b in
                                      (L0_gnn_gru_b_ih, L0_gnn_gru_b_hh)]).T),
    }
    nc = bacc.Bacc("TRN2", target_bir_lowering=False, num_devices=1)
    aps = {k: nc.dram_tensor("in_" + k, a.shape, mybir.dt.from_np(a.dtype), kind="ExternalInput").ap()
           for k, a in arrays.items()}
    out = nc.dram_tensor("out_0", (N, C), F32, kind="ExternalOutput").ap()
    gnn_program(nc, out=out, **aps)
    r = run_bass_kernel_spmd(nc, [{"in_" + k: a for k, a in arrays.items()}], core_ids=[0])
    return r.results[0]["out_0"]
```

```python
from contextlib import ExitStack

import concourse.bass as bass
from concourse import mybir

P = 128
BANK = 512
F32 = mybir.dt.float32
I32 = mybir.dt.int32
U32 = mybir.dt.uint32
ALU = mybir.AluOpType
ACT = mybir.ActivationFunctionType
AX_X = mybir.AxisListType.X

TPG = 5
GPS = 5
WIN = 64
QUADS = 4
QS = 32
CNT = 32
CREDIT = 16
META = 12
LN_EPS = 1e-5


def gnn_program(nc, x, x_t, src_tiles, dst, dst_tiles, ef_t, w1, b1, w2_oi, b2_oi,
                ih_t, hh_t, gate_b, out):
    N, C = x.shape
    FD, E = ef_t.shape
    HID = w1.shape[1]
    HA = HID + 1
    WC = C * C
    GE = TPG * P
    HE = GE // 2
    SE = GPS * GE
    TPS = TPG * GPS
    NSUB = E // SE
    NG = NSUB * GPS
    PAIRS, TAIL = NSUB // 2, NSUB % 2
    Q = N // QUADS
    RP = 125
    RJ = Q // RP
    ROUNDS = 2
    JW = BANK // P
    STEPS = [(RP * j, RP * min(JW, RJ - j), j, min(JW, RJ - j)) for j in range(0, RJ, JW)]
    GW = RP * JW
    NS = len(STEPS)
    assert PAIRS >= 2 and TAIL == 1
    assert E % SE == 0 and NSUB <= P and N % QUADS == 0 and Q % RP == 0 and C == 16

    def uses(rnd, par, i):
        per_round = PAIRS + (TAIL if par == 0 else 0)
        return i + (rnd * per_round + 1)

    table2 = nc.dram_tensor("h_rows", [N, C], F32, kind="Internal").ap()
    meta_d = nc.dram_tensor("meta_d", [NSUB, META], I32, kind="Internal").ap()
    base_d = nc.dram_tensor("base_d", [NSUB, GPS], F32, kind="Internal").ap()

    with ExitStack() as ctx:
        def sb(name, shape, dt=F32):
            return ctx.enter_context(nc.sbuf_tensor(name, shape, dt))

        def ps(name, shape):
            return ctx.enter_context(nc.psum_tensor(name, shape, F32))

        def sem(name):
            return ctx.enter_context(nc.semaphore(name))

        w1_sb = sb("w1_sb", [P, P])
        b1_sb = sb("b1_sb", [P, 1])
        w2_sb = sb("w2_sb", [P, WC])
        gate_w = sb("gate_w", [P, 4, P])
        bias = sb("bias", [P, 6])
        bias_rz = sb("bias_rz", [P, 2])
        ident = sb("ident", [P, P])
        win_iota = sb("win_iota", [P, WIN])
        eps = sb("eps", [P, 1])
        warm = sb("warm", [P, 1])
        dst_nat = sb("dst_nat", [P, SE], I32)
        dst_sb = sb("dst_sb", [P, NSUB * TPS], I32)
        base_all = sb("base_all", [P, NG])
        lo_hi = sb("lo_hi", [NSUB, 2, GPS])
        span = sb("span", [NSUB, GPS], I32)
        meta_w = sb("meta_w", [NSUB, META], I32)
        meta = sb("meta", [1, NSUB * META], I32)
        idx = sb("idx", [P, 2, TPS], I32)
        ef = sb("ef", [P, 2, SE])
        h_sb = sb("h_sb", [P, 2, GE])
        xg = sb("xg", [P, 2 * GPS, TPG, C])
        rel = sb("rel", [P, 2, TPS])
        prod = sb("prod", [P, 2, TPG, C, C])
        hot = sb("hot", [P, 2, TPG, WIN])
        msg = sb("msg", [P, 2 * GPS, TPG, CNT + C])
        rel_x = sb("rel_x", [P, TPG])
        hot_x = sb("hot_x", [P, TPG, WIN])
        acc = sb("acc", [CNT + C, N + WIN])
        mh = sb("mh", [P, Q])
        inv_q = dst_nat[:, 0:Q].bitcast(F32)
        r_q = sb("r_q", [P, 2, GW])
        z_q = sb("z_q", [P, 2, GW])
        t_q = sb("t_q", [P, 2, GW])
        n_q = sb("n_q", [P, 2, GW])
        rows = sb("rows", [RP, QUADS, RJ, C])
        xrows = sb("xrows", [RP, QUADS, RJ, C])
        cent = sb("cent", [RP, QUADS, RJ, C])
        stat = sb("stat", [RP, 4, QUADS, RJ])

        ps_w = ps("ps_w", [P, 6 * BANK])
        ps_h = ps("ps_h", [P, BANK])
        ps_a = ps("ps_a", [P, BANK])
        win_sum = ps_a[0:CNT + C, 0:WIN]
        R_BANK, Z_BANK, IN_BANK, HN_BANK, TR_BANK0 = (BANK * b for b in range(5))
        I_N, R, Z, H_N = range(4)

        def w_slot(s):
            return ps_w[:, s * 3 * BANK:s * 3 * BANK + TPG * WC]

        s_net = sem("s_net")
        s_gru = sem("s_gru")
        s_dst = sem("s_dst")
        s_xrows = sem("s_xrows")
        s_fill = sem("s_fill")
        s_ident = sem("s_ident")
        s_meta_w = sem("s_meta_w")
        s_meta = sem("s_meta")
        s_pro = sem("s_pro")
        s_ef = [sem(f"s_ef{p}") for p in range(2)]
        s_idx = [sem(f"s_idx{p}") for p in range(2)]
        s_xg = [sem(f"s_xg{k}") for k in range(2 * GPS)]
        s_h = sem("s_h")
        s_relu = sem("s_relu")
        s_w = sem("s_w")
        s_rel = sem("s_rel")
        s_prod = sem("s_prod")
        s_hot = sem("s_hot")
        s_msg = sem("s_msg")
        s_agg = sem("s_agg")
        s_acc = sem("s_acc")
        s_hot_x = sem("s_hot_x")
        s_agg_x = sem("s_agg_x")
        s_pack = sem("s_pack")
        s_cnt = sem("s_cnt")
        s_norm = sem("s_norm")
        s_gate = sem("s_gate")
        s_rz = sem("s_rz")
        s_pre = sem("s_pre")
        s_n = sem("s_n")
        s_new = sem("s_new")
        s_link = sem("s_link")
        s_tr = sem("s_tr")
        s_rows = sem("s_rows")
        s_table = sem("s_table")
        s_zero = sem("s_zero")
        s_ln = sem("s_ln")
        s_sd = sem("s_sd")
        s_y = sem("s_y")
        s_out = sem("s_out")

        NET_LOADS = 4
        GRU_LOADS = 4 * QUADS
        FILLED_EF, FILLED_NET, FILLED_GRU = 1, 2, 3

        def node_rows(table, c):
            off, w, _, jn = STEPS[c]
            return table.rearrange("(q n) c -> q n c", q=QUADS)[:, off:off + w, :].rearrange(
                "q (p j) c -> p q (j c)", j=jn)

        def step_rows(t, c):
            _, _, j, jn = STEPS[c]
            return t[:, :, j:j + jn, :]

        def step_bank(c):
            jn = STEPS[c][3]
            lo = TR_BANK0 + (c % 2) * BANK
            return ps_w[0:RP, lo:lo + jn * P].rearrange(
                "p (j q c) -> p q j c", q=QUADS, c=QS)[:, :, :, C:2 * C]

        block = ctx.enter_context(nc.Block())

        def for_subs(eng, emit, ahead=0):
            for i in range(ahead):
                emit(i, 0, False)
                emit(i, 1, False)
            with eng.Fori(ahead, PAIRS) as i:
                emit(i, 0, False)
                emit(i, 1, TAIL == 0)
            if TAIL:
                emit(PAIRS, 0, True)

        @block.sync
        def _(sp):
            for rnd in range(ROUNDS):
                if rnd > 0:
                    sp.wait_ge(s_h, 2 * rnd * NG + CREDIT)

                def emit(i, par, last, rnd=rnd):
                    sub = 2 * i + par
                    done = rnd * NG + (sub - 1) * GPS
                    for k in range(GPS):
                        sp.wait_ge(s_xg[par * GPS + k], 16 * TPG * (uses(rnd, par, i) - 1))
                    sp.dma_start(idx[:, par, :], src_tiles[bass.ds(sub * P, P), :]).then_inc(s_idx[par], 16)
                    sp.wait_ge(s_fill, FILLED_EF)
                    sp.wait_ge(s_h, done * 2 + CREDIT)
                    sp.dma_start(ef[0:FD, par, :], ef_t[:, bass.ds(sub * SE, SE)]).then_inc(s_ef[par], 16)

                for_subs(sp, emit, ahead=1)
            for c in range(NS):
                sp.dma_start(step_rows(xrows, c), node_rows(x, c)).then_inc(s_xrows, 16)
            sp.wait_ge(s_y, 1)
            for c in range(NS):
                sp.dma_start(node_rows(out, c), step_rows(rows, c)).then_inc(s_out, 16)
            sp.wait_ge(s_out, 16 * NS)
            sp.wait_ge(s_table, 16 * NS * (ROUNDS - 1))

        @block.gpsimd
        def _(pool):
            pool.memset(ident[:], 0.0)
            pool.iota(win_iota[:], [[1, WIN]], base=0, channel_multiplier=0,
                      allow_small_or_imprecise_dtypes=True)
            pool.drain()
            pool.affine_select(out=ident[:], in_=ident[:], compare_op=ALU.not_equal, fill=1.0, base=0,
                               pattern=[[-1, P]], channel_multiplier=1).then_inc(s_ident, 1)

            for rnd in range(ROUNDS):
                table = x if rnd == 0 else table2
                if rnd > 0:
                    pool.wait_ge(s_table, 16 * NS * rnd)

                def emit(i, par, last, rnd=rnd, table=table):
                    pool.wait_ge(s_idx[par], 16 * uses(rnd, par, i))
                    for k in range(GPS):
                        g = (2 * i + par) * GPS + k
                        pool.wait_ge(s_prod, rnd * NG + g - 2 * GPS + 1 + CREDIT)
                        pool.nop(nofuse=True)
                        for t in range(TPG):
                            pool.indirect_dma_start(
                                out=xg[:, par * GPS + k, t, :], out_offset=None, in_=table,
                                in_offset=bass.IndirectOffsetOnAxis(
                                    ap=idx[:, par, k * TPG + t:k * TPG + t + 1].bitcast(U32), axis=0),
                            ).then_inc(s_xg[par * GPS + k], 16)

                for_subs(pool, emit)
                if rnd < ROUNDS - 1:
                    for c, (off, w, _, _) in enumerate(STEPS):
                        pool.wait_ge(s_norm, NS * rnd + c + 1)
                        nodes = acc[:, 0:N].rearrange("a (q n) -> a q n", q=QUADS)[:, :, off:off + w]
                        pool.memset(nodes, 0.0).then_inc(s_zero, 1)
                    pool.memset(acc[:, N:N + WIN], 0.0).then_inc(s_zero, 1)

        @block.scalar
        def _(act):
            act.sem_inc(s_relu, CREDIT)
            act.wait_ge(s_idx[0], 16)
            act.dma_start(dst_nat[0:NSUB, :], dst.rearrange("(s e) -> s e", s=NSUB)).then_inc(s_dst, 16)
            act.dma_start(dst_sb[:], dst_tiles).then_inc(s_dst, 16)
            act.wait_ge(s_fill, FILLED_NET)
            act.dma_start(w1_sb[0:FD, 0:HID], w1).then_inc(s_net, 16)
            act.dma_start(b1_sb[0:HID, :], b1).then_inc(s_net, 16)
            act.dma_start(w2_sb[0:HID, :], w2_oi).then_inc(s_net, 16)
            act.dma_start(w2_sb[HID:HA, :], b2_oi).then_inc(s_net, 16)
            act.wait_ge(s_pro, 7)
            act.dma_start(meta_d, meta_w[:]).then_inc(s_meta_w, 16)
            act.dma_start(base_d, lo_hi[:, 0, :]).then_inc(s_meta_w, 16)
            act.wait_ge(s_meta_w, 32)
            act.dma_start(meta[:], meta_d.rearrange("s m -> (s m)").unsqueeze(0)).then_inc(s_meta, 16)
            act.dma_start(base_all[:], base_d.rearrange("s g -> (s g)").unsqueeze(0)
                          .to_broadcast([P, NG])).then_inc(s_meta, 16)
            act.wait_ge(s_fill, FILLED_GRU)
            for q in range(QUADS):
                lo = QS * q
                m_of, h_of = slice(lo, lo + C), slice(lo + C, lo + 2 * C)
                act.dma_start(gate_w[m_of, I_N:Z + 1, h_of], ih_t).then_inc(s_gru, 16)
                act.dma_start(gate_w[h_of, R:H_N + 1, h_of], hh_t).then_inc(s_gru, 16)
                act.dma_start(bias[h_of, :], gate_b).then_inc(s_gru, 16)
                act.dma_start(mh[h_of, :], x_t[:, q * Q:(q + 1) * Q]).then_inc(s_gru, 16)
            act.wait_ge(s_net, 16 * NET_LOADS)

            def pack(rnd, c):
                off, w, _, _ = STEPS[c]
                if rnd == 0:
                    for q in range(0, QUADS, 2):
                        last = act.copy(inv_q[QS * q:QS * q + C, off:off + w],
                                        acc[CNT:CNT + C, q * Q + off:q * Q + off + w])
                    last.then_inc(s_cnt, 1)
                for q in range(QUADS):
                    last = act.copy(mh[QS * q:QS * q + C, off:off + w],
                                    acc[0:C, q * Q + off:q * Q + off + w])
                last.then_inc(s_pack, 1)

            def to_rows(rnd, c):
                k = rnd * NS + c + 1
                act.wait_ge(s_tr, k)
                act.copy(step_rows(rows, c), step_bank(c)).then_inc(s_rows, 1)
                act.wait_ge(s_rows, k)
                act.dma_start(node_rows(table2, c), step_rows(rows, c)).then_inc(s_table, 16)

            for rnd in range(ROUNDS):
                def emit(i, par, last, rnd=rnd):
                    for k in range(GPS):
                        g = (2 * i + par) * GPS + k
                        act.wait_ge(s_w, rnd * NG + g - 1 + CREDIT)
                        for half in range(2):
                            act.wait_ge(s_h, (rnd * NG + g) * 2 + half + 1 + CREDIT)
                            act.activation(h_sb[:, (par * GPS + k) % 2, half * HE:(half + 1) * HE],
                                           ps_h[:, 0:HE], ACT.Relu,
                                           bias=b1_sb[:, 0:1]).then_inc(s_relu, 1)

                for_subs(act, emit)
                act.wait_ge(s_gru, 16 * GRU_LOADS)
                act.activation(warm[:], bias[:, 0:1], ACT.Sigmoid)
                act.wait_ge(s_acc, NG * (rnd + 1) + CREDIT + rnd + 1)
                pack(rnd, 0)
                pack(rnd, 1)
                for c, (off, w, _, _) in enumerate(STEPS):
                    k = rnd * NS + c
                    act.wait_ge(s_gate, 2 * k + 1)
                    act.wait_ge(s_new, k - 1 if c else 0)
                    act.activation(r_q[:, c % 2, 0:w], ps_w[:, R_BANK:R_BANK + w], ACT.Sigmoid,
                                   bias=bias_rz[:, 0:1])
                    act.activation(z_q[:, c % 2, 0:w], ps_w[:, Z_BANK:Z_BANK + w], ACT.Sigmoid,
                                   bias=bias_rz[:, 1:2]).then_inc(s_rz, 1)
                    if c + 2 < NS:
                        pack(rnd, c + 2)
                    act.wait_ge(s_pre, k + 1)
                    act.activation(n_q[:, c % 2, 0:w], t_q[:, c % 2, 0:w], ACT.Tanh,
                                   bias=bias[:, 2:3]).then_inc(s_n, 1)
                    if c > 0 and rnd < ROUNDS - 1:
                        to_rows(rnd, c - 1)
                if rnd < ROUNDS - 1:
                    to_rows(rnd, NS - 1)
            act.wait_ge(s_ln, 1)
            act.activation(stat[:, 2], stat[:, 1], ACT.Sqrt, bias=eps[0:RP, :],
                           scale=1.0 / C).then_inc(s_sd, 1)

        @block.tensor
        def _(pe):
            pe.sem_inc(s_h, CREDIT)
            pe.sem_inc(s_w, CREDIT)
            pe.sem_inc(s_agg, CREDIT)
            pe.wait_ge(s_net, 16 * NET_LOADS)
            pe.wait_ge(s_meta, 32)
            seen_x = pe.alloc_register("seen_x")
            pe.reg_mov(seen_x, 0)

            def hidden(rnd, g, half, at, i):
                par, k = at // GPS, at % GPS
                if k == 0 and half == 0:
                    pe.wait_ge(s_ef[par], 16 * uses(rnd, par, i))
                pe.wait_ge(s_relu, (rnd * NG + g) * 2 + half + CREDIT)
                lo = k * GE + half * HE
                pe.matmul(ps_h[:, 0:HE], w1_sb[:], ef[:, par, lo:lo + HE],
                          start=True, stop=True).then_inc(s_h, 1)

            def weights(rnd, g, slot, tiles):
                if tiles[0] == 0:
                    pe.wait_ge(s_prod, rnd * NG + g - 1 + CREDIT)
                    pe.wait_ge(s_relu, (rnd * NG + g) * 2 + 2 + CREDIT)
                for t in tiles:
                    last = pe.matmul(w_slot(slot)[:, t * WC:(t + 1) * WC], h_sb[:, slot, t * P:(t + 1) * P],
                                     w2_sb[:], start=True, stop=True)
                if tiles[-1] == TPG - 1:
                    last.then_inc(s_w, 1)

            def window_sum(messages, one_hot):
                for t in range(TPG):
                    last = pe.matmul(win_sum, messages[:, t, :], one_hot[:, t, :],
                                     start=(t == 0), stop=(t == TPG - 1))
                return last

            for rnd in range(ROUNDS):
                if rnd > 0:
                    pe.wait_ge(s_rows, NS * rnd)
                hidden(rnd, 0, 0, 0, 0)
                hidden(rnd, 0, 1, 0, 0)
                hidden(rnd, 1, 0, 1, 0)
                weights(rnd, 0, 0, range(TPG))
                hidden(rnd, 1, 1, 1, 0)

                def emit(i, par, last, rnd=rnd):
                    for k in range(GPS):
                        g = (2 * i + par) * GPS + k
                        at = par * GPS + k
                        nxt, i_nxt = (at + 2) % (2 * GPS), i + (at + 2) // (2 * GPS)
                        for half in range(2):
                            if not (last and k + 2 >= GPS):
                                hidden(rnd, g + 2, half, nxt, i_nxt)
                            if not (last and k + 1 >= GPS):
                                weights(rnd, g + 1, (at + 1) % 2, (range(0, 3), range(3, TPG))[half])
                        pe.wait_ge(s_hot, rnd * NG + g + 1)
                        pe.wait_ge(s_msg, rnd * NG + g + 1)
                        pe.wait_ge(s_acc, rnd * NG + g + CREDIT + rnd)
                        window_sum(msg[:, at], hot[:, at % 2]).then_inc(s_agg, 1)
                    sub = 2 * i + par
                    more = pe.value_load(meta[0:1, bass.ds(sub * META + 2 * GPS, 1)],
                                         min_val=0, max_val=N // WIN)
                    with pe.If(more > 0):
                        for k in range(GPS):
                            n_x = pe.value_load(meta[0:1, bass.ds(sub * META + GPS + k, 1)],
                                                min_val=0, max_val=N // WIN)
                            with pe.If(n_x > 0):
                                with pe.Fori(0, n_x):
                                    pe.reg_add(seen_x, seen_x, 1)
                                    pe.wait_ge(s_hot_x, seen_x)
                                    window_sum(msg[:, par * GPS + k], hot_x).then_inc(s_agg_x, 1)

                for_subs(pe, emit)

                pe.wait_ge(s_gru, 16 * GRU_LOADS)
                pe.wait_ge(s_ident, 1)

                def transposes(c):
                    off, w, _, jn = STEPS[c]
                    pe.wait_ge(s_new, rnd * NS + c + 1)
                    if c >= 2:
                        pe.wait_ge(s_rows, rnd * NS + c - 1)
                    for j in range(jn):
                        col = TR_BANK0 + (c % 2) * BANK + j * P
                        nodes = mh[:, off:off + w].rearrange("c (p j) -> c j p", j=jn)[:, j, :]
                        last = pe.matmul(ps_w[0:RP, col:col + P], nodes, ident[:], start=True, stop=True)
                    last.then_inc(s_tr, 1)

                for c, (off, w, _, _) in enumerate(STEPS):
                    k = rnd * NS + c
                    pe.wait_ge(s_norm, k + 1)
                    pe.wait_ge(s_rz, k)

                    def gate(g, lo, both=mh[:, off:off + w], w=w):
                        return pe.matmul(ps_w[:, lo:lo + w], gate_w[:, g, :], both, start=True, stop=True)

                    gate(R, R_BANK)
                    gate(Z, Z_BANK).then_inc(s_gate, 1)
                    pe.wait_ge(s_pre, k)
                    gate(I_N, IN_BANK)
                    gate(H_N, HN_BANK).then_inc(s_gate, 1)
                    if c > 0:
                        transposes(c - 1)
                transposes(NS - 1)

        @block.vector
        def _(dve):
            links = [0]

            def link(ins):
                links[0] += 1
                ins.then_inc(s_link, 1)
                dve.wait_ge(s_link, links[0])

            dve.sem_inc(s_prod, CREDIT)
            dve.sem_inc(s_acc, CREDIT)
            dve.memset(ef[:], 0.0)
            dve.drain().then_inc(s_fill, 1)
            for t in (w1_sb, w2_sb, b1_sb):
                dve.memset(t[:], 0.0)
            dve.drain()
            dve.memset(b1_sb[HID:HA, :], 1.0)
            dve.drain().then_inc(s_fill, 1)
            dve.wait_ge(s_dst, 32)
            by_group = dst_nat[0:NSUB, :].rearrange("s (g e) -> s g e", g=GPS)
            dve.tensor_reduce(lo_hi[:, 0, :], by_group, AX_X, ALU.min).then_inc(s_pro, 1)
            dve.tensor_reduce(lo_hi[:, 1, :], by_group, AX_X, ALU.max).then_inc(s_pro, 1)
            dve.memset(meta_w[:], 0).then_inc(s_pro, 1)
            dve.wait_ge(s_pro, 3)
            dve.tensor_tensor(span[:], lo_hi[:, 1, :], lo_hi[:, 0, :], ALU.subtract).then_inc(s_pro, 1)
            dve.tensor_copy(meta_w[:, 0:GPS], lo_hi[:, 0, :]).then_inc(s_pro, 1)
            dve.wait_ge(s_pro, 5)
            dve.tensor_scalar(meta_w[:, GPS:2 * GPS], span[:], WIN.bit_length() - 1, None,
                              ALU.logical_shift_right).then_inc(s_pro, 1)
            dve.wait_ge(s_pro, 6)
            dve.tensor_reduce(meta_w[:, 2 * GPS:2 * GPS + 1], meta_w[:, GPS:2 * GPS], AX_X,
                              ALU.max).then_inc(s_pro, 1)
            for t in (gate_w, bias, mh):
                dve.memset(t[:], 0.0)
            dve.drain().then_inc(s_fill, 1)
            dve.memset(eps[:], LN_EPS)
            dve.memset(msg[:, :, :, C:CNT + C], 1.0)
            dve.memset(acc[:], 0.0)
            dve.memset(inv_q, 1.0)
            dve.drain()
            dve.wait_ge(s_ident, 1)
            dve.wait_ge(s_meta, 32)
            seen_x = dve.alloc_register("seen_x")
            dve.reg_mov(seen_x, 0)
            start_x = dve.alloc_register("start_x")
            iota_b = win_iota[:].unsqueeze(1).to_broadcast([P, TPG, WIN])

            def products(rnd, g, at, i):
                par = at // GPS
                dve.wait_ge(s_w, rnd * NG + g + 1 + CREDIT)
                dve.wait_ge(s_xg[at], 16 * TPG * uses(rnd, par, i))
                w = w_slot(at % 2).rearrange("p (t o i) -> p t o i", t=TPG, o=C)
                xb = xg[:, at].unsqueeze(2).to_broadcast([P, TPG, C, C])
                dve.tensor_tensor(prod[:, at % 2], w, xb, ALU.mult).then_inc(s_prod, 1)

            def relative(rnd, sub, i, par):
                dve.tensor_tensor(
                    rel[:, par, :].rearrange("p (g t) -> p g t", g=GPS),
                    dst_sb[:, bass.ds(sub * TPS, TPS)].rearrange("p (g t) -> p g t", g=GPS),
                    base_all[:, bass.ds(sub * GPS, GPS)].unsqueeze(2).to_broadcast([P, GPS, TPG]),
                    ALU.subtract).then_inc(s_rel, 1)

            def one_hot(to, of):
                return dve.tensor_tensor(to, iota_b, of.unsqueeze(2).to_broadcast([P, TPG, WIN]),
                                         ALU.is_equal)

            for rnd in range(ROUNDS):
                if rnd > 0:
                    dve.wait_ge(s_zero, (NS + 1) * rnd)
                products(rnd, 0, 0, 0)

                def emit(i, par, last, rnd=rnd):
                    sub = 2 * i + par
                    relative(rnd, sub, i, par)
                    dve.wait_ge(s_rel, rnd * NSUB + sub + 1)
                    for k in range(GPS):
                        g = sub * GPS + k
                        at = par * GPS + k
                        start = dve.value_load(meta[0:1, bass.ds(sub * META + k, 1)],
                                               min_val=0, max_val=N - 1)
                        dve.wait_ge(s_agg, rnd * NG + g - 1 + CREDIT)
                        one_hot(hot[:, at % 2], rel[:, par, k * TPG:(k + 1) * TPG]).then_inc(s_hot, 1)
                        dve.wait_ge(s_prod, rnd * NG + g + 1 + CREDIT)
                        dve.tensor_reduce(msg[:, at, :, 0:C], prod[:, at % 2], AX_X, ALU.add).then_inc(s_msg, 1)
                        if not (last and k == GPS - 1):
                            dve.wait_ge(s_msg, rnd * NG + g)
                            products(rnd, g + 1, (at + 1) % (2 * GPS), i + (at + 1) // (2 * GPS))
                        dve.wait_ge(s_agg, rnd * NG + g + 1 + CREDIT)
                        dve.wait_ge(s_acc, rnd * NG + g + CREDIT + rnd)
                        window = acc[:, bass.ds(start, WIN)]
                        dve.tensor_tensor(window, window, win_sum, ALU.add).then_inc(s_acc, 1)
                    more = dve.value_load(meta[0:1, bass.ds(sub * META + 2 * GPS, 1)],
                                          min_val=0, max_val=N // WIN)
                    with dve.If(more > 0):
                        for k in range(GPS):
                            n_x = dve.value_load(meta[0:1, bass.ds(sub * META + GPS + k, 1)],
                                                 min_val=0, max_val=N // WIN)
                            with dve.If(n_x > 0):
                                start = dve.value_load(meta[0:1, bass.ds(sub * META + k, 1)],
                                                       min_val=0, max_val=N - 1)
                                dve.tensor_copy(rel_x[:], rel[:, par, k * TPG:(k + 1) * TPG])
                                dve.drain()
                                dve.reg_mov(start_x, start)
                                with dve.Fori(0, n_x):
                                    dve.tensor_scalar(rel_x[:], rel_x[:], -float(WIN), None, ALU.add)
                                    dve.drain()
                                    one_hot(hot_x[:], rel_x[:]).then_inc(s_hot_x, 1)
                                    dve.reg_add(seen_x, seen_x, 1)
                                    dve.wait_ge(s_agg_x, seen_x)
                                    dve.reg_add(start_x, start_x, WIN)
                                    at_x = dve.snap(start_x, min_val=0, max_val=N - 1)
                                    window = acc[:, bass.ds(at_x, WIN)]
                                    dve.tensor_tensor(window, window, win_sum, ALU.add)
                                    dve.drain()

                for_subs(dve, emit)
                dve.drain().then_inc(s_acc, 1)

                def mean(c):
                    off, w, _, _ = STEPS[c]
                    both, inv = mh[:, off:off + w], inv_q[:, off:off + w]
                    if rnd == 0:
                        for q in range(1, QUADS, 2):
                            last = dve.tensor_copy(inv_q[QS * q:QS * q + C, off:off + w],
                                                   acc[CNT:CNT + C, q * Q + off:q * Q + off + w])
                        link(last)
                        dve.wait_ge(s_cnt, c + 1)
                        link(dve.tensor_scalar(inv, inv, 1.0, None, ALU.max))
                        link(dve.reciprocal(inv, inv))
                    dve.wait_ge(s_pack, rnd * NS + c + 1)
                    dve.tensor_tensor(both, both, inv, ALU.mult).then_inc(s_norm, 1)

                def before_n(c):
                    w = STEPS[c][1]
                    r, t = r_q[:, c % 2, 0:w], t_q[:, c % 2, 0:w]
                    dve.wait_ge(s_rz, rnd * NS + c + 1)
                    dve.wait_ge(s_gate, 2 * (rnd * NS + c + 1))
                    link(dve.scalar_tensor_tensor(out=t, in0=ps_w[:, HN_BANK:HN_BANK + w],
                                                  scalar=bias[:, 5:6], in1=r, op0=ALU.add, op1=ALU.mult))
                    dve.tensor_tensor(t, t, ps_w[:, IN_BANK:IN_BANK + w], ALU.add).then_inc(s_pre, 1)

                def new_h(c):
                    off, w, _, _ = STEPS[c]
                    z, t, n, h = z_q[:, c % 2, 0:w], t_q[:, c % 2, 0:w], n_q[:, c % 2, 0:w], mh[:, off:off + w]
                    dve.wait_ge(s_n, rnd * NS + c + 1)
                    link(dve.tensor_tensor(t, h, n, ALU.subtract))
                    link(dve.tensor_tensor(t, t, z, ALU.mult))
                    dve.tensor_tensor(h, n, t, ALU.add).then_inc(s_new, 1)

                def residual(c):
                    _, _, j, jn = STEPS[c]
                    y, d = step_rows(rows, c), step_rows(cent, c)
                    total, squares = (stat[:, m, :, j:j + jn] for m in range(2))
                    dve.wait_ge(s_tr, rnd * NS + c + 1)
                    dve.tensor_tensor(y, step_bank(c), step_rows(xrows, c), ALU.add).then_inc(s_rows, 1)
                    dve.wait_ge(s_rows, rnd * NS + c + 1)
                    link(dve.tensor_reduce(total, y, AX_X, ALU.add))
                    link(dve.tensor_scalar(total, total, 1.0 / C, None, ALU.mult))
                    mean_b = total.unsqueeze(3).to_broadcast([RP, QUADS, jn, C])
                    link(dve.tensor_tensor(d, y, mean_b, ALU.subtract))
                    link(dve.tensor_tensor(y, d, d, ALU.mult))
                    link(dve.tensor_reduce(squares, y, AX_X, ALU.add))

                if rnd == 0:
                    dve.wait_ge(s_gru, 16 * GRU_LOADS)
                    link(dve.tensor_tensor(bias_rz[:], bias[:, 0:2], bias[:, 3:5], ALU.add))
                if rnd == ROUNDS - 1:
                    dve.wait_ge(s_xrows, 16 * NS)
                    dve.wait_ge(s_table, 16 * NS * rnd)
                mean(0)
                mean(1)
                for c in range(NS):
                    before_n(c)
                    if c + 2 < NS:
                        mean(c + 2)
                    new_h(c)
                    if c > 0 and rnd == ROUNDS - 1:
                        residual(c - 1)
                if rnd == ROUNDS - 1:
                    residual(NS - 1)

            dve.sem_inc(s_ln, 1)
            dve.wait_ge(s_sd, 1)
            link(dve.reciprocal(stat[:, 3], stat[:, 2]))
            dve.tensor_tensor(rows[:], cent[:], stat[:, 3].unsqueeze(3).to_broadcast([RP, QUADS, RJ, C]),
                              ALU.mult).then_inc(s_y, 1)


def kernel(x, src, dst, edge_attr_13, L0_gnn_fnet_w1, L0_gnn_fnet_b1, L0_gnn_fnet_w2, L0_gnn_fnet_b2,
           L0_gnn_gru_w_ih, L0_gnn_gru_w_hh, L0_gnn_gru_b_ih, L0_gnn_gru_b_hh):
    import numpy as np
    import concourse.bacc as bacc
    from concourse.bass_utils import run_bass_kernel_spmd

    def lay(a):
        return np.ascontiguousarray(a)

    N, C = x.shape
    E, FD = edge_attr_13.shape
    HID = L0_gnn_fnet_w1.shape[1]
    TPS = TPG * GPS

    def tiles(a):
        return np.asarray(a).reshape(-1, TPS, P).transpose(0, 2, 1)

    arrays = {
        "x": lay(x),
        "x_t": lay(np.asarray(x).T),
        "src_tiles": lay(tiles(src).reshape(-1, TPS)),
        "dst": lay(dst),
        "dst_tiles": lay(tiles(dst).transpose(1, 0, 2).reshape(P, -1)),
        "ef_t": lay(np.asarray(edge_attr_13).T),
        "w1": lay(L0_gnn_fnet_w1),
        "b1": lay(np.asarray(L0_gnn_fnet_b1).reshape(HID, 1)),
        "w2_oi": lay(np.asarray(L0_gnn_fnet_w2).reshape(HID, C, C).transpose(0, 2, 1).reshape(HID, C * C)),
        "b2_oi": lay(np.asarray(L0_gnn_fnet_b2).reshape(1, C, C).transpose(0, 2, 1).reshape(1, C * C)),
        "ih_t": lay(np.roll(np.asarray(L0_gnn_gru_w_ih).reshape(3, C, C), 1, axis=0).transpose(2, 0, 1)),
        "hh_t": lay(np.asarray(L0_gnn_gru_w_hh).reshape(3, C, C).transpose(2, 0, 1)),
        "gate_b": lay(np.concatenate([np.asarray(b).reshape(3, C) for b in
                                      (L0_gnn_gru_b_ih, L0_gnn_gru_b_hh)]).T),
    }
    nc = bacc.Bacc("TRN2", target_bir_lowering=False, num_devices=1)
    aps = {k: nc.dram_tensor("in_" + k, a.shape, mybir.dt.from_np(a.dtype), kind="ExternalInput").ap()
           for k, a in arrays.items()}
    out = nc.dram_tensor("out_0", (N, C), F32, kind="ExternalOutput").ap()
    gnn_program(nc, out=out, **aps)
    r = run_bass_kernel_spmd(nc, [{"in_" + k: a for k, a in arrays.items()}], core_ids=[0])
    return r.results[0]["out_0"]
```
